# Optimizing a Trainium2 kernel written in Bass

```python
import numpy as np
import jax
import jax.numpy as jnp

def _softmax(x, axis=-1):
    return jax.nn.softmax(x, axis=axis)

def _gelu(x):
    return jax.nn.gelu(x, approximate=True)

def _silu(x):
    return jax.nn.silu(x)

def _sigmoid(x):
    return jax.nn.sigmoid(x)

def _layernorm(x, axis=-1, eps=1e-05):
    m = jnp.mean(x, axis=axis, keepdims=True)
    v = jnp.var(x, axis=axis, keepdims=True)
    return (x - m) / jnp.sqrt(v + eps)

def _scatter_add(tgt, idx, src, axis=0):
    return tgt.at[idx].add(src)

def _segment_sum(src, seg, n):
    return jax.ops.segment_sum(src, seg, n)
kernel_name = 'mk_adaln_d1_jaxref_r8_998096'

def setup_inputs(seed: int=0):
    np.random.seed(seed)
    _w = jnp.asarray

    def _L0_attn_setup():
        import jax, jax.numpy as jnp
        import numpy as np
        D_MODEL = 128
        NUM_HEADS = 16
        D_K = D_MODEL // NUM_HEADS
        ROPE_THETA = 10000.0

        def _apply_rope(t):
            S, dk = (t.shape[-2], t.shape[-1])
            inv_freq = 1.0 / ROPE_THETA ** (jnp.arange(0, dk, 2) / dk)
            angles = jnp.outer(jnp.arange(S), inv_freq)
            cos = jnp.repeat(jnp.cos(angles), 2, axis=-1).astype(t.dtype)
            sin = jnp.repeat(jnp.sin(angles), 2, axis=-1).astype(t.dtype)
            t_even = t[..., 0::2]
            t_odd = t[..., 1::2]
            t_rot = jnp.stack([-t_odd, t_even], axis=-1).reshape(t.shape)
            return t * cos + t_rot * sin
        key = jax.random.key(seed)
        kx, kq, kk, kv, ko = jax.random.split(key, 5)
        B, S = (4, 256)
        std = (2.0 / (D_MODEL + D_MODEL)) ** 0.5

        def w(k):
            return jax.random.truncated_normal(k, -3.0, 3.0, (D_MODEL, D_MODEL), jnp.float32) * std
        return {'x': jax.random.normal(kx, (B, S, D_MODEL), jnp.float32), 'Wq': w(kq), 'Wk': w(kk), 'Wv': w(kv), 'Wo': w(ko)}
    _L0_attn_in = _L0_attn_setup()

    def _L0_ffn_setup():
        import jax, jax.numpy as jnp
        import numpy as np
        import math
        N_EXP = 8
        TOP_K = 2
        CAPACITY_FACTOR = 1.25

        def _capacity(num_tokens):
            cap = math.floor(TOP_K * CAPACITY_FACTOR * num_tokens / N_EXP)
            cap += cap % 2
            return int(cap)
        key = jax.random.key(seed)
        k1, k2, k3, k4 = jax.random.split(key, 4)
        B, C, d = (4, 128, 128)
        x = jax.random.normal(k1, (B, C, d), dtype=jnp.float32)
        w_g = jax.random.normal(k2, (d, N_EXP), dtype=jnp.float32) * 0.02
        c_fc = jax.random.normal(k3, (N_EXP, d, 4 * d), dtype=jnp.float32) * 0.02
        c_proj = jax.random.normal(k4, (N_EXP, 4 * d, d), dtype=jnp.float32) * 0.02
        return {'x': x, 'w_g': w_g, 'c_fc': c_fc, 'c_proj': c_proj}
    _L0_ffn_in = _L0_ffn_setup()
    _L0_c = _w((lambda *s: np.random.randn(*s).astype(np.float32) * 0.05)(1, 128))
    _L0_wmod = _w((lambda *s: np.random.randn(*s).astype(np.float32) * 0.05)(128, 6 * 128) * 128 ** (-0.5))
    _d = {'L0_attn_x': _L0_attn_in['x'], 'L0_attn_Wq': _L0_attn_in['Wq'], 'L0_attn_Wk': _L0_attn_in['Wk'], 'L0_attn_Wv': _L0_attn_in['Wv'], 'L0_attn_Wo': _L0_attn_in['Wo'], 'L0_ffn_w_g': _L0_ffn_in['w_g'], 'L0_ffn_c_fc': _L0_ffn_in['c_fc'], 'L0_ffn_c_proj': _L0_ffn_in['c_proj'], 'L0_c': _L0_c, 'L0_wmod': _L0_wmod}
    _x0 = _d['L0_attn_x']
    _d['L0_attn_x'] = jax.random.normal(jax.random.fold_in(jax.random.key(seed), 1), (1, 2048, 128), dtype=_x0.dtype)
    del _x0
    return _d

def reference(L0_attn_x, L0_attn_Wq, L0_attn_Wk, L0_attn_Wv, L0_attn_Wo, L0_ffn_w_g, L0_ffn_c_fc, L0_ffn_c_proj, L0_c, L0_wmod):

    def _L0_attn_ref(x, Wq, Wk, Wv, Wo):
        import jax, jax.numpy as jnp
        import numpy as np
        D_MODEL = 128
        NUM_HEADS = 16
        D_K = D_MODEL // NUM_HEADS
        ROPE_THETA = 10000.0

        def _apply_rope(t):
            S, dk = (t.shape[-2], t.shape[-1])
            inv_freq = 1.0 / ROPE_THETA ** (jnp.arange(0, dk, 2) / dk)
            angles = jnp.outer(jnp.arange(S), inv_freq)
            cos = jnp.repeat(jnp.cos(angles), 2, axis=-1).astype(t.dtype)
            sin = jnp.repeat(jnp.sin(angles), 2, axis=-1).astype(t.dtype)
            t_even = t[..., 0::2]
            t_odd = t[..., 1::2]
            t_rot = jnp.stack([-t_odd, t_even], axis=-1).reshape(t.shape)
            return t * cos + t_rot * sin
        B, S, D = x.shape
        H, dk = (NUM_HEADS, D_K)
        q = jnp.einsum('bsi,io->bso', x, Wq).reshape(B, S, H, dk).swapaxes(1, 2)
        k = jnp.einsum('bsi,io->bso', x, Wk).reshape(B, S, H, dk).swapaxes(1, 2)
        v = jnp.einsum('bsi,io->bso', x, Wv).reshape(B, S, H, dk).swapaxes(1, 2)
        q = _apply_rope(q)
        k = _apply_rope(k)
        scores = jnp.einsum('bhqd,bhkd->bhqk', q, k) / dk ** 0.5
        causal = jnp.tril(jnp.ones((S, S), dtype=bool))
        scores = jnp.where(causal, scores, -jnp.inf)
        attn = jax.nn.softmax(scores, axis=-1)
        out = jnp.einsum('bhqk,bhkd->bhqd', attn, v)
        out = out.swapaxes(1, 2).reshape(B, S, D)
        return jnp.einsum('bsi,io->bso', out, Wo)

    def _L0_ffn_ref(x, w_g, c_fc, c_proj):
        import jax, jax.numpy as jnp
        import numpy as np
        import math
        N_EXP = 8
        TOP_K = 2
        CAPACITY_FACTOR = 1.25

        def _capacity(num_tokens):
            cap = math.floor(TOP_K * CAPACITY_FACTOR * num_tokens / N_EXP)
            cap += cap % 2
            return int(cap)
        B, C, d = x.shape
        T = B * C
        cap = _capacity(T)
        xt = x.reshape(T, d)
        logits = xt @ w_g
        top_v, top_i = jax.lax.top_k(logits, TOP_K)
        full = jnp.full_like(logits, -jnp.inf)
        full = full.at[jnp.arange(T)[:, None], top_i].set(top_v)
        probs = jax.nn.softmax(full, axis=-1)
        exp_mask = jax.nn.one_hot(top_i, N_EXP, dtype=jnp.int32)
        exp_mask = jnp.transpose(exp_mask, (1, 0, 2))
        exp_rank = jnp.cumsum(exp_mask.reshape(TOP_K * T, N_EXP), axis=0) - 1
        exp_rank = exp_rank.reshape(TOP_K, T, N_EXP)
        exp_mask = exp_mask * (exp_rank < cap).astype(jnp.int32)
        exp_rank = jnp.sum(exp_mask * exp_rank, axis=-1)
        exp_weights = exp_mask.astype(x.dtype) * probs[None]
        rank_oh = jax.nn.one_hot(exp_rank, cap, dtype=x.dtype)
        cb_weight = jnp.einsum('kte,ktc->tec', exp_weights, rank_oh)
        sec_mask = (cb_weight != 0).astype(x.dtype)
        exp_batches = jnp.einsum('tec,td->ecd', sec_mask, xt)
        h = jax.nn.gelu(jnp.einsum('ecd,edf->ecf', exp_batches, c_fc), approximate=False)
        exp_out = jnp.einsum('ecf,efd->ecd', h, c_proj)
        out = cb_weight.reshape(T, N_EXP * cap) @ exp_out.reshape(N_EXP * cap, d)
        return out.reshape(B, C, d)
    x = L0_attn_x
    mod = (_silu(L0_c) @ L0_wmod).reshape(L0_c.shape[0], 6, 1, -1)
    sa, ca, ga, sb, cb, gb = (mod[:, 0], mod[:, 1], mod[:, 2], mod[:, 3], mod[:, 4], mod[:, 5])
    ga = (2 * (ga >= 0) - 1) * jnp.maximum(jnp.abs(ga), 0.25)
    gb = (2 * (gb >= 0) - 1) * jnp.maximum(jnp.abs(gb), 0.25)
    h = _layernorm(x, axis=-1) * (1 + ca) + sa
    x = x + ga * _L0_attn_ref(h, L0_attn_Wq, L0_attn_Wk, L0_attn_Wv, L0_attn_Wo)
    h = _layernorm(x, axis=-1) * (1 + cb) + sb
    x = x + gb * _L0_ffn_ref(h, L0_ffn_w_g, L0_ffn_c_fc, L0_ffn_c_proj)
    return x

_drawn_inputs = setup_inputs


def setup_inputs(seed=0):
    import zlib

    import numpy as np

    out = dict(_drawn_inputs(seed))
    spreads = {}
    factors = {'L0_attn_Wq': 2.929,
     'L0_attn_Wk': 2.835,
     'L0_ffn_w_g': 6.83,
     'L0_ffn_c_fc': 6.067,
     'L0_ffn_c_proj': 5.962}
    for name, (base, spread) in spreads.items():
        noise = np.random.default_rng([zlib.crc32(name.encode()), seed]).standard_normal(out[name].shape)
        drawn = base * np.exp(spread * noise) if base else spread * noise
        out[name] = jnp.asarray(drawn.astype(out[name].dtype))
    for name, factor in factors.items():
        out[name] = (out[name] * factor).astype(out[name].dtype)
    return out
```

```python
import numpy as np
import concourse.bass as bass
from concourse import mybir
from contextlib import ExitStack

P = 128
S = 2048
D = 128
H = 16
DK = D // H
NT = S // P
QB = 512
NB = S // QB
TB = QB // P
GH = 4
NG = H // GH
NU = NB * NG
NPAIR = H // 2
E = 8
TOPK = 2
F = 4 * D
NF = F // P
CAP = 2 * int(1.25 * S) // E
CT = CAP // P
NSLOT = E * CAP
SCALE = float(DK) ** -0.5
EPS = 1e-5

TERMS = [(0, 0), (0, 1), (1, 0), (1, 1), (0, 2), (2, 0)]
ROWS = DK * len(TERMS)
KROWS = ROWS + 3
MW = 1024
PR = 12
AVLAG = 2


def units():
    return [(b, g) for b in range(NB) for g in range(NG)]


def max_pieces(u):
    b, _ = units()[u]
    return [(j, i, k0, min(MW, P * (i + 1) - k0))
            for j in range(GH) for i in range(TB * b, TB * (b + 1)) for k0 in range(0, P * (i + 1), MW)]


def make_plan():
    plan = [("mod", 0)] + [("xt", b) for b in range(NB)]
    for b in range(NB):
        plan += [("q", b), ("k", b), ("v", b)]
    cost_m = lambda p: p[3] + 60
    size_s = [GH * sum(QB - P * max(0, kt - TB * b) for kt in range(TB * (b + 1))) for b, _ in units()]
    size_m = [sum(cost_m(p) for p in max_pieces(u)) for u in range(NU)]
    pieces = [(u, n) for u in range(NU) for n in range(len(max_pieces(u)))]
    at = 0
    done = 0.0
    later = []

    def tick():
        for x in later:
            x[0] -= 1
        while later and later[0][0] <= 0:
            plan.append(later.pop(0)[1])

    def piece():
        nonlocal at, done
        u, n = pieces[at]
        plan.append(("max", u, n))
        done += cost_m(max_pieces(u)[n])
        at += 1
        tick()
        if n == len(max_pieces(u)) - 1:
            plan.append(("maxend", u))
            later.append([3, ("negmax", u)])
            later.sort(key=lambda x: x[0])

    def up_to(u):
        while at < len(pieces) and pieces[at][0] <= u:
            piece()

    cum_m = [0]
    for x in size_m:
        cum_m.append(cum_m[-1] + x)
    cum_s = [0]
    for x in size_s:
        cum_s.append(cum_s[-1] + x)
    up_to(0)
    avs = []
    for u, (b, g) in enumerate(units()):
        up_to(u)
        while ("negmax", u) not in plan:
            if at < len(pieces) and pieces[at][0] <= u + 1:
                piece()
            else:
                plan.append(later.pop(0)[1])
        rate, base = 0.0, done
        for v in range(u + 1, NU):
            rate = max(rate, (cum_m[v + 1] - done) / (max(cum_s[v] - 5000, cum_s[u] + size_s[u] * 0.5) - cum_s[u]))
        went = 0
        for kt in range(TB * (b + 1)):
            plan.append(("scores", u, kt))
            avs.append((u, kt))
            went += GH * (QB - P * max(0, kt - TB * b))
            tick()
            while at < len(pieces) and done < base + rate * went and pieces[at][0] <= u + 3:
                piece()
            while len(avs) > AVLAG:
                plan.append(("av",) + avs.pop(0))
                uu, kk = plan[-1][1:]
                if kk == TB * (units()[uu][0] + 1) - 1:
                    plan.append(("evac", uu))
                    if uu % NG == NG - 1:
                        bb = uu // NG
                        for n, s in enumerate([("norm", bb, 0), ("norm", bb, 1), ("ot", bb, 0), ("ot", bb, 1),
                                               ("wo", bb, 0), ("wo", bb, 1), ("h2t", bb), ("logit", bb)]):
                            later.append([2 + 2 * n, s])
                        later.sort(key=lambda x: x[0])
    for uu, kk in avs:
        plan.append(("av", uu, kk))
    plan.append(("evac", NU - 1))
    plan += [x[1] for x in later]
    bb = NB - 1
    plan += [("norm", bb, 0), ("norm", bb, 1), ("ot", bb, 0), ("ot", bb, 1), ("wo", bb, 0), ("wo", bb, 1),
             ("h2t", bb), ("logit", bb), ("rank", 0)]
    return plan


class Steps:

    def __init__(self):
        self.plan = make_plan()
        ringless = ("scores", "av", "evac", "maxend")
        self.ring = {s: n for n, s in enumerate(x for x in self.plan if x[0] not in ringless)}
        self.nth = {}
        count = {}
        for s in self.plan:
            self.nth[s] = count.get(s[0], 0)
            count[s[0]] = self.nth[s] + 1
        self.tile = {}
        for s in self.plan:
            if s[0] == "scores":
                for j in range(GH):
                    self.tile[s[1], s[2], j] = len(self.tile)
        self.diag = {}
        for s in self.plan:
            if s[0] == "scores":
                for j in range(GH):
                    if s[2] >= TB * units()[s[1]][0]:
                        self.diag[s[1], s[2], j] = len(self.diag) + 1


def first_column(u, kt):
    return P * max(0, kt - TB * units()[u][0])


def block_kernel(nc, x, Wq, Wk, Wv, Wo, w_g, c_fc, c_proj, c, wmod, cos_t, sin_t, ones_t, out):
    f32, bf16, u32 = mybir.dt.float32, mybir.dt.bfloat16, mybir.dt.uint32
    ALU, ACT, AX = mybir.AluOpType, mybir.ActivationFunctionType, mybir.AxisListType
    st = Steps()
    plan, ring, nth = st.plan, st.ring, st.nth
    NRING = len(ring)

    q_rows = nc.dram_tensor("q_rows", (H, ROWS, S), bf16)
    k_rows = nc.dram_tensor("k_rows", (H, ROWS, S), bf16)
    m_rows = nc.dram_tensor("m_rows", (NU, 3 * TB * GH, P), bf16)
    slots_x = nc.dram_tensor("slots_x", (NSLOT, D), f32)
    slots_y = nc.dram_tensor("slots_y", (NSLOT, D), f32)

    ctx = ExitStack()
    with ctx:
        def sb(name, shape, dt=f32):
            return ctx.enter_context(nc.sbuf_tensor(name, shape, dt))

        def sem(name):
            return ctx.enter_context(nc.semaphore(name))

        X = sb("X", [P, NT, D])
        XN = sb("XN", [P, NT, D])
        hT = sb("hT", [P, S])
        QS = sb("QS", [P, NPAIR, S], bf16)
        KS = sb("KS", [P, NPAIR, S], bf16)
        VX = sb("VX", [P, NT, H, DK + 1])
        PRB = sb("PRB", [P, PR, QB])
        part_sets = [PRB[:, PR // 2:PR, :].rearrange("p a b -> p (a b)").bitcast(bf16),
                     sb("parts23", [P, 4 * 3 * QB], bf16)[:, :]]
        part_views = [a.rearrange("p (w b r n) -> p w b r n", w=2, b=2, r=3) for a in part_sets]
        CS = sb("CS", [P, 2, S])
        W1 = CS[:, :, :].rearrange("p a s -> p (a s)").rearrange("p (e f) -> p e f", e=E)
        W2 = sb("W2", [P, E, NF, D])
        OT = sb("OT", [P, NG, QB])
        RT = sb("RT", [P, 2, 3, QB])
        wsb = sb("wsb", [P, 6, D])
        wg = sb("wg", [P, E])
        wm = sb("wm", [P, 6 * D])
        MODB = sb("MODB", [P, 6, D])
        modT = sb("modT", [P, 2])
        ccol = sb("ccol", [P, 4])
        silu_b = sb("silu_b", [P, P])
        stats = sb("stats", [P, NT, 6])
        mv = sb("mv", [P, 2, NT, 2])
        veps = sb("veps", [P, NT])
        half = sb("half", [P, NT])
        rstd = sb("rstd", [P, 2, NT])
        ident = sb("ident", [P, P])
        identb = sb("identb", [P, P], bf16)
        causal = sb("causal", [P, P], bf16)
        before = sb("before", [P, P])
        ones = sb("ones", [P, P])
        mpart = sb("mpart", [P, 2, NU, GH * TB])
        mx = sb("mx", [P, NU, GH * TB])
        nm = sb("nm", [P, 2, 3, GH * TB])
        nmp = sb("nmp", [P, NU, 3, GH * TB], bf16)
        mrow = sb("mrow", [3 * GH * TB, 2, P], bf16)
        rl = sb("rl", [P, 2, H])
        LG = sb("LG", [P, NT, E])
        T8 = sb("T8", [P, NT, 8])
        I8 = sb("I8", [P, NT, 8], u32)
        idxf = sb("idxf", [P, TOPK, NT])
        io = sb("io", [P, E])
        tables = part_sets[1].bitcast(f32)[:, 0:3 * E * TOPK * NT].rearrange("p (a e n) -> p a e n", a=3, e=E)
        OH = tables[:, 0].rearrange("p e (k t) -> p e k t", k=TOPK)
        incl, restart = tables[:, 1], tables[:, 2]
        rk = sb("rk", [P, TOPK * NT])
        keep = sb("keep", [P, TOPK * NT])
        slotf = sb("slotf", [P, 3, TOPK * NT])
        put_at = sb("put_at", [P, TOPK * NT], u32)
        get_at = sb("get_at", [P, TOPK * NT], u32)
        wt = sb("wt", [P, 5, NT])
        wk_ = sb("wk_", [P, TOPK, NT])
        rt_flat = RT[:, :, :, :].rearrange("p a b n -> p (a b n)")
        zeros = rt_flat[:, 0:CAP]
        On = rt_flat[:, 2 * QB:3 * QB].rearrange("p (n d) -> p n d", n=2)
        OnT = rt_flat[:, 3 * QB:4 * QB].rearrange("p (n d) -> p n d", n=2)
        flat = KS[:, :, :].rearrange("p a s -> p (a s)").bitcast(f32)
        XB = flat[:, 0:2 * CAP].rearrange("p (n t d) -> p n t d", n=2, t=CT)
        XBT = flat[:, 2 * CAP:4 * CAP].rearrange("p (n s) -> p n s", n=2)
        YB = flat[:, 4 * CAP:6 * CAP].rearrange("p (n t d) -> p n t d", n=2, t=CT)
        flatq = QS[:, :, :].rearrange("p a s -> p (a s)").bitcast(f32)
        HG = flatq[:, 0:2 * NF * CAP].rearrange("p (n f s) -> p n f s", n=2, f=NF)
        GY = PRB[:, :, :].rearrange("p a b -> p (a b)")[:, 0:TOPK * NT * D].rearrange("p (n d) -> p n d", d=D)

        WK = [ctx.enter_context(nc.psum_tensor(f"work{i}", [P, 2 * QB], f32)) for i in range(2)]
        SC = [ctx.enter_context(nc.psum_tensor(f"score{i}", [P, QB], f32)) for i in range(2)]
        AV = [ctx.enter_context(nc.psum_tensor(f"av{i}", [P, QB], f32)) for i in range(2)]

        x_in, w_in, mod_in, rope_in, ones_in, w2_in, w1_in = (
            sem(n) for n in ("x_in", "w_in", "mod_in", "rope_in", "ones_in", "w2_in", "w1_in"))
        wg_in, zero_out = sem("wg_in"), sem("zero_out")
        qk_put = [sem(f"qk_put{b}") for b in range(NB)]
        qk_got = [sem(f"qk_got{b}") for b in range(NB)]
        m_put, m_got = [sem(f"m_put{i}") for i in range(2)], [sem(f"m_got{i}") for i in range(2)]
        const_ok = sem("const_ok")
        pool_step = sem("pool_step")
        dve_step = sem("dve_step")
        dve_const = sem("dve_const")
        act_silu = sem("act_silu")
        silu_ok = sem("silu_ok")
        rot_ok = sem("rot_ok")
        stats_ok, rstd_ok, xn_ok = sem("stats_ok"), sem("rstd_ok"), sem("xn_ok")
        modt_ok, modb_ok = sem("modt_ok"), sem("modb_ok")
        full = [sem(f"full{i}") for i in range(2)]
        free = [sem(f"free{i}") for i in range(2)]
        ht_ok, vx_ok, roped, kparts_ok, qparts_ok = (
            sem(n) for n in ("ht_ok", "vx_ok", "roped", "kparts_ok", "qparts_ok"))
        max_ok, mx_ok, nmp_ok, mrow_ok = sem("max_ok"), sem("mx_ok"), sem("nmp_ok"), sem("mrow_ok")
        scored, exped, masked, av_ok, evaced = (
            sem(n) for n in ("scored", "exped", "masked", "av_ok", "evaced"))
        on_ok, ont_ok, x2_ok, stats2_ok, xn2_ok, h2_ok, h2t_ok, logit_ok = (
            sem(n) for n in ("on_ok", "ont_ok", "x2_ok", "stats2_ok", "xn2_ok", "h2_ok", "h2t_ok", "logit_ok"))
        norm_read, h2t_read = sem("norm_read"), sem("h2t_read")
        wo_ok, w2_ok = sem("wo_ok"), sem("w2_ok")
        top_ok, diff_ok, ediff_ok, oh_ok, idx_ok, wts_ok = (
            sem(n) for n in ("top_ok", "diff_ok", "ediff_ok", "oh_ok", "idx_ok", "wts_ok"))
        scattered, restart_ok = sem("scattered"), sem("restart_ok")
        xb_in = [sem(f"xb_in{i}") for i in range(2)]
        xbt_ps, xbt_ok = sem("xbt_ps"), sem("xbt_ok")
        up_full, up_free = [sem(f"up_full{i}") for i in range(2)], [sem(f"up_free{i}") for i in range(2)]
        down_ps, yb_ok = sem("down_ps"), sem("yb_ok")
        yb_out = [sem(f"yb_out{i}") for i in range(2)]
        gathered = [sem(f"gathered{i}") for i in range(NT)]
        sum_ok, out_ok, out_done = sem("sum_ok"), sem("out_ok"), sem("out_done")

        block = ctx.enter_context(nc.Block())

        def wait_full(eng, step):
            eng.wait_ge(full[ring[step] % 2], ring[step] // 2 + 1)
            return WK[ring[step] % 2]

        def parts(which, b, r):
            return part_views[b // 2][:, which, b % 2, r, :]

        def prev(s):
            return (s[1] - 1, s[2])

        def release(eng, s):
            eng.sem_inc(free[ring[s] % 2], 1)

        sign = RT[:, 0, 0, 0:D]

        @block.sync
        def _(sp):
            x_t = x[0].rearrange("(t p) d -> p t d", p=P)
            for b in range(NB):
                sp.dma_start(X[:, TB * b:TB * (b + 1), :], x_t[:, TB * b:TB * (b + 1), :]).then_inc(x_in, 16)
            sp.dma_start(ccol[:, 0:1], c.rearrange("a p -> p a")).then_inc(mod_in, 16)
            sp.dma_start(wm[:, :], wmod).then_inc(mod_in, 16)
            for n, w in enumerate((Wq, Wk, Wv, Wo)):
                sp.dma_start(wsb[:, n, :], w).then_inc(w_in, 16)
            sp.dma_start(CS[:, 0, :], cos_t).then_inc(rope_in, 16)
            sp.dma_start(CS[:, 1, :], sin_t).then_inc(rope_in, 16)
            for par in range(2):
                sp.dma_start(KS[64 * par + ROWS:64 * par + KROWS, :, :],
                             ones_t.rearrange("r (a s) -> r a s", a=NPAIR)).then_inc(ones_in, 16)
            sp.dma_start(wg[:, :], w_g).then_inc(wg_in, 16)

            def expand(b):
                cols = slice(QB * b, QB * (b + 1))
                sp.wait_ge(qparts_ok, b + 1)
                for t, (a, _) in enumerate(TERMS):
                    sp.dma_start(q_rows[:, DK * t:DK * (t + 1), cols], parts(0, b, a)).then_inc(qk_put[b], 16)
                sp.wait_ge(kparts_ok, b + 1)
                for t, (_, a) in enumerate(TERMS):
                    sp.dma_start(k_rows[:, DK * t:DK * (t + 1), cols], parts(1, b, a)).then_inc(qk_put[b], 16)
                sp.wait_ge(qk_put[b], 16 * 2 * len(TERMS))
                for rows, dst in ((q_rows, QS), (k_rows, KS)):
                    by_pair = rows.ap().rearrange("(a b) r s -> b r a s", b=2)
                    for par in range(2):
                        sp.dma_start(dst[64 * par:64 * par + ROWS, :, cols],
                                     by_pair[par, :, :, cols]).then_inc(qk_got[b], 16)

            def put_negmax(u):
                b, g = units()[u]
                sp.wait_ge(mrow_ok, u + 1)
                sp.dma_start(m_rows[u], mrow[:, u % 2, :]).then_inc(m_put[u % 2], 16)
                sp.wait_ge(m_put[u % 2], 16 * (u // 2 + 1))
                src = m_rows[u].rearrange("(r a b i) q -> b r a (i q)", r=3, a=2, b=2)
                for par in range(2):
                    sp.dma_start(QS[64 * par + ROWS:64 * par + KROWS, 2 * g:2 * g + 2, QB * b:QB * (b + 1)],
                                 src[par]).then_inc(m_got[u % 2], 16)

            expand(0)
            sp.dma_start(W2[:, :, :, :], c_proj.rearrange("e (f p) d -> p e f d", p=P)).then_inc(w2_in, 16)
            expand(1)
            sp.wait_ge(roped, 2 * NB)
            sp.dma_start(W1, c_fc.rearrange("e d f -> d e f")).then_inc(w1_in, 16)
            sp.wait_ge(const_ok, 1)
            put_negmax(0)
            expand(2)
            expand(3)
            put_negmax(1)
            sp.wait_ge(dve_const, 2)
            for e in range(E):
                sp.dma_start(slots_x[e * CAP:(e + 1) * CAP, :].rearrange("(p t) d -> p (t d)", p=P),
                             zeros).then_inc(zero_out, 16)
            for u in range(2, NU):
                put_negmax(u)

            sp.wait_ge(scattered, 16 * TOPK * NT)
            for e in range(E + 1):
                if e < E:
                    if e >= 2:
                        sp.wait_ge(xbt_ps, e - 1)
                    sp.dma_start(XB[:, e % 2], slots_x[e * CAP:(e + 1) * CAP, :]
                                 .rearrange("(t p) d -> p t d", p=P)).then_inc(xb_in[e % 2], 16)
                if e >= 1:
                    sp.wait_ge(yb_ok, e)
                    sp.dma_start(slots_y[(e - 1) * CAP:e * CAP, :].rearrange("(t p) d -> p t d", p=P),
                                 YB[:, (e - 1) % 2]).then_inc(yb_out[(e - 1) % 2], 16)
            out_t = out[0].rearrange("(t p) d -> p t d", p=P)
            for b in range(NB):
                sp.wait_ge(out_ok, TB * (b + 1))
                sp.dma_start(out_t[:, TB * b:TB * (b + 1), :], X[:, TB * b:TB * (b + 1), :]).then_inc(out_done, 16)
            sp.wait_ge(out_done, 16 * NB)

        @block.gpsimd
        def _(pool):
            g = nc.gpsimd
            n = [0]

            def chain(ins):
                n[0] += 1
                ins.then_inc(pool_step, 1)
                pool.wait_ge(pool_step, n[0])

            g.memset(half[:, :], -0.5).then_inc(pool_step, 1)
            g.memset(ones[:, :], 1.0).then_inc(pool_step, 1)
            g.memset(ident[:, :], 0.0).then_inc(pool_step, 1)
            g.memset(identb[:, :], 0.0).then_inc(pool_step, 1)
            g.memset(causal[:, :], 0.0).then_inc(pool_step, 1)
            n[0] = 5
            pool.wait_ge(pool_step, n[0])
            for m in (ident, identb):
                g.affine_select(out=m[:, :], in_=m[:, :], compare_op=ALU.not_equal, fill=1.0, base=0,
                                pattern=[[-1, P]], channel_multiplier=1).then_inc(pool_step, 1)
            g.affine_select(out=causal[:, :], in_=causal[:, :], compare_op=ALU.is_ge, fill=-1e30, base=0,
                            pattern=[[-1, P]], channel_multiplier=1).then_inc(pool_step, 1)
            g.affine_select(out=before[:, :], in_=ones[:, :], compare_op=ALU.is_gt, fill=0.0, base=0,
                            pattern=[[1, P]], channel_multiplier=-1).then_inc(pool_step, 1)
            g.memset(VX[:, :, :, DK:DK + 1], 1.0).then_inc(pool_step, 1)
            n[0] += 5
            chain(g.iota(I8[:, 0, :], pattern=[[1, E]], base=0, channel_multiplier=0))
            chain(g.tensor_copy(io[:, :], I8[:, 0, :]))
            pool.sem_inc(const_ok, 1)

            def rstd_of(which, tiles):
                chain(g.tensor_scalar(veps[:, tiles], mv[:, which, tiles, 1], EPS, None, ALU.add))
                g.tensor_tensor(rstd[:, which, tiles], veps[:, tiles], half[:, tiles], ALU.pow).then_inc(rstd_ok, 1)

            pool.wait_ge(stats_ok, 1)
            rstd_of(0, slice(0, NT))
            for b in range(NB):
                pool.wait_ge(roped, 2 * b + 2)
                r, d1 = RT[:, 1, 2, :], RT[:, 1, 0, :]
                chain(g.tensor_scalar(parts(1, b, 0), r, 1.0, 1.0, ALU.mult, ALU.mult))
                chain(g.tensor_tensor(d1, r, parts(1, b, 0), ALU.subtract))
                chain(g.tensor_scalar(parts(1, b, 1), d1, 1.0, 1.0, ALU.mult, ALU.mult))
                chain(g.tensor_tensor(r, d1, parts(1, b, 1), ALU.subtract))
                g.tensor_scalar(parts(1, b, 2), r, 1.0, 1.0, ALU.mult, ALU.mult).then_inc(kparts_ok, 1)
            pool.wait_ge(modb_ok, 1)
            pool.wait_ge(w_in, 16 * 4)
            g.tensor_tensor(wsb[:, 3, :], wsb[:, 3, :], MODB[:, 2, :], ALU.mult).then_inc(wo_ok, 1)
            pool.wait_ge(w2_in, 16)
            gates = 0
            for s in plan:
                if s[0] == "maxend":
                    u = s[1]
                    pool.wait_ge(mx_ok, u + 1)
                    chain(g.tensor_scalar(nm[:, u % 2, 0, :], mx[:, u, :], -1.0, 1.0, ALU.mult, ALU.mult))
                    chain(g.tensor_copy(nmp[:, u, 0, :], nm[:, u % 2, 0, :]))
                    chain(g.tensor_tensor(nm[:, u % 2, 1, :], nm[:, u % 2, 0, :], nmp[:, u, 0, :], ALU.subtract))
                    chain(g.tensor_copy(nmp[:, u, 1, :], nm[:, u % 2, 1, :]))
                    chain(g.tensor_tensor(nm[:, u % 2, 2, :], nm[:, u % 2, 1, :], nmp[:, u, 1, :], ALU.subtract))
                    g.tensor_copy(nmp[:, u, 2, :], nm[:, u % 2, 2, :]).then_inc(nmp_ok, 1)
                elif s[0] == "scores":
                    _, u, kt = s
                    if kt >= TB * units()[u][0]:
                        q0 = first_column(u, kt)
                        for j in range(GH):
                            t = st.tile[u, kt, j]
                            pool.wait_ge(exped, t + 1)
                            tile = PRB[:, t % PR, q0:q0 + P]
                            g.affine_select(out=tile, in_=tile, compare_op=ALU.is_ge, fill=0.0, base=0,
                                            pattern=[[1, P]], channel_multiplier=-1).then_inc(masked, 1)
                    elif gates < E:
                        g.tensor_tensor(W2[:, gates], W2[:, gates],
                                        MODB[:, 5:6, :].to_broadcast([P, NF, D]), ALU.mult).then_inc(w2_ok, 1)
                        gates += 1
                elif s[0] == "h2t":
                    b = s[1]
                    tiles = slice(TB * b, TB * (b + 1))
                    if b == 0:
                        pool.wait_ge(qk_put[NB - 1], 16 * 2 * len(TERMS))
                        chain(g.memset(restart, 1.0))
                        g.memset(restart[:, :, 0:1], 0.0).then_inc(restart_ok, 1)
                    pool.wait_ge(stats2_ok, b + 1)
                    rstd_of(1, tiles)
                    pool.wait_ge(xn2_ok, b + 1)
                    chain(g.tensor_tensor(XN[:, tiles, :], XN[:, tiles, :],
                                          MODB[:, 4:5, :].to_broadcast([P, TB, D]), ALU.mult))
                    g.tensor_tensor(XN[:, tiles, :], XN[:, tiles, :],
                                    MODB[:, 3:4, :].to_broadcast([P, TB, D]), ALU.add).then_inc(h2_ok, 1)
            pool.wait_ge(idx_ok, 1)
            pool.wait_ge(h2_ok, NB)
            pool.wait_ge(zero_out, 16 * E)
            for k in range(TOPK):
                for t in range(NT):
                    m = k * NT + t
                    g.indirect_dma_start(out=slots_x[:, :],
                                         out_offset=bass.IndirectOffsetOnAxis(ap=put_at[:, m:m + 1], axis=0),
                                         in_=XN[:, t, :], in_offset=None, bounds_check=NSLOT - 1,
                                         oob_is_err=False).then_inc(scattered, 16)
            for i in range(2):
                pool.wait_ge(yb_out[i], 16 * E // 2)
            for t in range(NT):
                for k in range(TOPK):
                    m = k * NT + t
                    g.indirect_dma_start(out=GY[:, TOPK * t + k, :], out_offset=None, in_=slots_y[:, :],
                                         in_offset=bass.IndirectOffsetOnAxis(ap=get_at[:, m:m + 1], axis=0),
                                         bounds_check=NSLOT - 1, oob_is_err=False).then_inc(gathered[t], 16)

        @block.scalar
        def _(act):
            a = nc.scalar
            act.wait_ge(mod_in, 32)
            a.activation(ccol[:, 1:2], ccol[:, 0:1], ACT.Exp, scale=-1.0).then_inc(act_silu, 1)
            for s in plan:
                if s[0] == "xt":
                    b = s[1]
                    w = wait_full(act, s)
                    act.wait_ge(modt_ok, 2)
                    a.activation(hT[:, QB * b:QB * (b + 1)], w[:, 0:QB], ACT.Identity, bias=modT[:, 0:1],
                                 scale=modT[:, 1:2]).then_inc(free[ring[s] % 2], 1)
                elif s[0] == "v":
                    b = s[1]
                    w = wait_full(act, s)
                    act.wait_ge(const_ok, 1)
                    a.activation(VX[:, TB * b:TB * (b + 1), :, 0:DK],
                                 w[:, 0:QB].rearrange("p (t h d) -> p t h d", t=TB, h=H),
                                 ACT.Copy).then_inc(free[ring[s] % 2], 1)
                elif s[0] == "negmax":
                    u = s[1]
                    w = wait_full(act, s)
                    if u >= 2:
                        act.wait_ge(m_put[u % 2], 16 * (u // 2))
                    a.activation(mrow[:, u % 2, :], w[0:3 * GH * TB, 0:P // 2].bitcast(bf16),
                                 ACT.Copy).then_inc(free[ring[s] % 2], 1)
                    act.wait_ge(free[ring[s] % 2], ring[s] // 2 + 1)
                    act.sem_inc(mrow_ok, 1)
                elif s[0] == "scores":
                    _, u, kt = s
                    q0 = first_column(u, kt)
                    for j in range(GH):
                        t = st.tile[u, kt, j]
                        act.wait_ge(scored, t + 1)
                        if t == PR // 2:
                            for i in range(2):
                                act.wait_ge(qk_put[i], 16 * 2 * len(TERMS))
                        if t >= PR:
                            act.wait_ge(av_ok, (t - PR) // GH + 1)
                        a.activation(PRB[:, t % PR, q0:QB], SC[t % 2][:, q0:QB], ACT.Exp,
                                     scale=SCALE).then_inc(exped, 1)
                elif s[0] == "evac":
                    u = s[1]
                    b, g = units()[u]
                    act.wait_ge(av_ok, sum(TB * (bb + 1) for bb, _ in units()[:u + 1]))
                    if b >= 1:
                        act.wait_ge(norm_read, 2 * b)
                    a.activation(OT[:, g, :], AV[u % 2][:, :], ACT.Copy).then_inc(evaced, 1)
                elif s[0] == "ot":
                    w = wait_full(act, s)
                    if nth[s] >= 2:
                        act.wait_ge(full[ring[("wo",) + prev(s)] % 2], ring[("wo",) + prev(s)] // 2 + 1)
                    a.activation(OnT[:, nth[s] % 2, :], w[:, 0:2 * P], ACT.Copy).then_inc(free[ring[s] % 2], 1)
                elif s[0] == "h2t":
                    w = wait_full(act, s)
                    a.activation(hT[:, QB * s[1]:QB * (s[1] + 1)], w[:, 0:QB], ACT.Copy).then_inc(free[ring[s] % 2], 1)
            act.wait_ge(diff_ok, 1)
            a.activation(wt[:, 1, :], wt[:, 0, :], ACT.Exp).then_inc(ediff_ok, 1)
            for e in range(E):
                for f in range(NF):
                    m = e * NF + f
                    act.wait_ge(up_full[m % 2], m // 2 + 1)
                    if e >= 2 and f == 0:
                        act.wait_ge(down_ps, e - 1)
                    a.activation(HG[:, e % 2, f, :].rearrange("p (n s) -> p n s", n=2),
                                 WK[m % 2][:, :].rearrange("p (n s) -> p n s", n=2)[:, :, 0:CAP // 2],
                                 ACT.Gelu).then_inc(up_free[m % 2], 1)

        @block.vector
        def _(dve):
            v = nc.vector
            n = [0]

            def chain(ins):
                n[0] += 1
                ins.then_inc(dve_step, 1)
                dve.wait_ge(dve_step, n[0])

            for i in range(2):
                v.memset(AV[i][:, :], 0.0).then_inc(dve_const, 1)
            for t in range(NT):
                if t == 0:
                    dve.wait_ge(x_in, 16 * NB)
                v.bn_stats(stats[:, t, :], X[:, t, :]).then_inc(dve_step, 1)
            n[0] += NT
            dve.wait_ge(dve_step, n[0])
            for t in range(NT):
                ins = v.bn_aggr(mv[:, 0, t, :], stats[:, t, :]).then_inc(dve_step, 1)
                n[0] += 1
            dve.wait_ge(dve_step, n[0])
            dve.sem_inc(stats_ok, 1)
            dve.wait_ge(act_silu, 1)
            chain(v.tensor_scalar(ccol[:, 2:3], ccol[:, 1:2], 1.0, None, ALU.add))
            chain(v.reciprocal(ccol[:, 3:4], ccol[:, 2:3]))
            chain(v.tensor_tensor(ccol[:, 1:2], ccol[:, 0:1], ccol[:, 3:4], ALU.mult))
            v.tensor_copy(silu_b[:, :], ccol[:, 1:2].to_broadcast([P, P])).then_inc(silu_ok, 1)
            dve.wait_ge(rstd_ok, 1)
            for t in range(NT):
                v.tensor_scalar(XN[:, t, :], X[:, t, :], mv[:, 0, t, 0:1], rstd[:, 0, t:t + 1],
                                ALU.subtract, ALU.mult).then_inc(xn_ok, 1)
            dve.wait_ge(w_in, 16 * 4)
            for i in range(2):
                src = wsb[:, i, :].rearrange("p (n two) -> p n two", two=2)
                dst = wsb[:, 4 + i, :].rearrange("p (n two) -> p n two", two=2)
                v.tensor_scalar(dst[:, :, 0], src[:, :, 1], -1.0, None, ALU.mult).then_inc(rot_ok, 1)
                v.tensor_copy(dst[:, :, 1], src[:, :, 0]).then_inc(rot_ok, 1)

            for s in plan:
                kind = s[0]
                if kind == "mod":
                    w = wait_full(dve, s)
                    v.tensor_copy(modT[:, 0:1], w[:, 6 * D:6 * D + 1]).then_inc(modt_ok, 1)
                    v.tensor_scalar(modT[:, 1:2], w[:, 6 * D + 1:6 * D + 2], 1.0, None, ALU.add).then_inc(modt_ok, 1)
                    chain(v.tensor_copy(MODB[:, :, :].rearrange("p a d -> p (a d)"), w[:, 0:6 * D]))
                    for i in (2, 5):
                        chain(v.tensor_scalar(sign, MODB[:, i, :], 0.0, 2.0, ALU.is_ge, ALU.mult))
                        chain(v.tensor_scalar(sign, sign, -1.0, None, ALU.add))
                        chain(v.tensor_tensor(MODB[:, i, :], MODB[:, i, :], sign, ALU.mult))
                        chain(v.tensor_scalar(MODB[:, i, :], MODB[:, i, :], 0.25, None, ALU.max))
                        chain(v.tensor_tensor(MODB[:, i, :], MODB[:, i, :], sign, ALU.mult))
                    chain(v.tensor_scalar(MODB[:, 4, :], MODB[:, 4, :], 1.0, None, ALU.add))
                    dve.sem_inc(modb_ok, 1)
                    release(dve, s)
                elif kind in ("q", "k"):
                    b, i = s[1], kind == "k"
                    w = wait_full(dve, s)
                    dve.wait_ge(rope_in, 32)
                    if i and b:
                        dve.wait_ge(kparts_ok, b)
                    cols = slice(QB * b, QB * (b + 1))
                    v.tensor_tensor(RT[:, i, 0, :], w[:, 0:QB], CS[:, 0, cols], ALU.mult).then_inc(dve_step, 1)
                    n[0] += 1
                    chain(v.tensor_tensor(RT[:, i, 1, :], w[:, QB:2 * QB], CS[:, 1, cols], ALU.mult))
                    release(dve, s)
                    r, d1 = RT[:, i, 2, :], RT[:, i, 0, :]
                    v.tensor_tensor(r, RT[:, i, 0, :], RT[:, i, 1, :], ALU.add).then_inc(roped, 1)
                    if not i:
                        dve.wait_ge(roped, 2 * b + 1)
                        chain(v.tensor_copy(parts(0, b, 0), r))
                        chain(v.tensor_tensor(d1, r, parts(0, b, 0), ALU.subtract))
                        chain(v.tensor_copy(parts(0, b, 1), d1))
                        chain(v.tensor_tensor(r, d1, parts(0, b, 1), ALU.subtract))
                        v.tensor_copy(parts(0, b, 2), r).then_inc(qparts_ok, 1)
                        dve.wait_ge(qparts_ok, b + 1)
                    else:
                        if b == NB - 1:
                            dve.wait_ge(kparts_ok, NB)
                            v.memset(zeros, 0.0).then_inc(dve_const, 1)
                elif kind == "max":
                    _, u, m = s
                    j, i, k0, keys = max_pieces(u)[m]
                    w = wait_full(dve, s)
                    col = j * TB + i % TB
                    v.reduce_max(mpart[:, k0 // MW, u, col:col + 1], w[:, 0:keys], AX.X).then_inc(free[ring[s] % 2], 1)
                elif kind == "maxend":
                    u = s[1]
                    last = max(ring[p] for p in (("max", u, m) for m in range(len(max_pieces(u)))))
                    for slot in range(2):
                        upto = last if last % 2 == slot else last - 1
                        dve.wait_ge(free[slot], upto // 2 + 1)
                    second = mpart[:, 1 if units()[u][0] * QB >= MW else 0, u, :]
                    v.tensor_tensor(mx[:, u, :], mpart[:, 0, u, :], second, ALU.max).then_inc(mx_ok, 1)
                elif kind == "norm":
                    i = nth[s] % 2
                    w = wait_full(dve, s)
                    strips = w[:, :].rearrange("p (t h r) -> p t h r", t=2, h=H)
                    if nth[s] >= 2:
                        dve.wait_ge(full[ring[("ot",) + prev(s)] % 2], ring[("ot",) + prev(s)] // 2 + 1)
                    for t in range(2):
                        v.reciprocal(rl[:, t, :], strips[:, t, :, DK]).then_inc(dve_step, 1)
                        n[0] += 1
                    dve.wait_ge(dve_step, n[0])
                    for t in range(2):
                        ins = v.tensor_tensor(On[:, i, t * D:(t + 1) * D].rearrange("p (h d) -> p h d", h=H),
                                              strips[:, t, :, 0:DK],
                                              rl[:, t, :].rearrange("p (h o) -> p h o", o=1).to_broadcast([P, H, DK]),
                                              ALU.mult).then_inc(on_ok, 1)
                    dve.wait_ge(on_ok, 2 * (nth[s] + 1))
                    release(dve, s)
                elif kind == "wo":
                    _, b, h2 = s
                    t0 = TB * b + 2 * h2
                    w = wait_full(dve, s)
                    v.tensor_tensor(X[:, t0:t0 + 2, :], w[:, 0:2 * D].rearrange("p (t d) -> p t d", t=2),
                                    X[:, t0:t0 + 2, :], ALU.add).then_inc(x2_ok, 1)
                    dve.wait_ge(x2_ok, nth[s] + 1)
                    release(dve, s)
                    for t in range(t0, t0 + 2):
                        chain(v.bn_stats(stats[:, t, :], X[:, t, :]))
                    for t in range(t0, t0 + 2):
                        chain(v.bn_aggr(mv[:, 1, t, :], stats[:, t, :]))
                    if h2 == 1:
                        dve.sem_inc(stats2_ok, 1)
                elif kind == "h2t":
                    b = s[1]
                    dve.wait_ge(rstd_ok, b + 2)
                    for t in range(TB * b, TB * (b + 1)):
                        chain(v.tensor_scalar(XN[:, t, :], X[:, t, :], mv[:, 1, t, 0:1], rstd[:, 1, t:t + 1],
                                              ALU.subtract, ALU.mult))
                    dve.sem_inc(xn2_ok, 1)
                elif kind == "logit":
                    b = s[1]
                    w = wait_full(dve, s)
                    chain(v.tensor_copy(LG[:, TB * b:TB * (b + 1), :],
                                        w[:, 0:TB * E].rearrange("p (t e) -> p t e", t=TB)))
                    release(dve, s)
                    for t in range(TB * b, TB * (b + 1)):
                        v.max(T8[:, t, :], LG[:, t, :]).then_inc(dve_step, 1)
                    n[0] += TB
                    dve.wait_ge(dve_step, n[0])
                    for t in range(TB * b, TB * (b + 1)):
                        v.max_index(I8[:, t, :], T8[:, t, :], LG[:, t, :]).then_inc(dve_step, 1)
                    n[0] += TB
                    dve.wait_ge(dve_step, n[0])
                elif kind == "rank":
                    v.tensor_tensor(wt[:, 0, :], T8[:, :, 1], T8[:, :, 0], ALU.subtract).then_inc(diff_ok, 1)
                    for k in range(TOPK):
                        chain(v.tensor_copy(idxf[:, k, :], I8[:, :, k]))
                    flat_idx = idxf[:, :, :].rearrange("p k t -> p (k t)")
                    for e in range(E):
                        v.tensor_scalar(OH[:, e].rearrange("p k t -> p (k t)"), flat_idx, io[:, e:e + 1], None,
                                        ALU.is_equal).then_inc(oh_ok, 1)
                    w = wait_full(dve, s)
                    dve.wait_ge(restart_ok, 1)
                    n_oh = E * TOPK * NT
                    local, total = w[:, 0:n_oh], w[:, QB:QB + n_oh]
                    fl = incl.rearrange("p e n -> p (e n)")
                    chain(v.tensor_tensor_scan(fl, restart.rearrange("p e n -> p (e n)"), total, 0.0,
                                               ALU.mult, ALU.add))
                    chain(v.tensor_tensor(fl, fl, total, ALU.subtract))
                    chain(v.tensor_tensor(fl, fl, local, ALU.add))
                    chain(v.tensor_tensor(fl, fl, OH.rearrange("p e k t -> p (e k t)"), ALU.mult))
                    release(dve, s)
                    chain(v.tensor_reduce(rk[:, :], incl.rearrange("p e n -> p n e"), AX.X, ALU.add))
                    chain(v.tensor_scalar(keep[:, :], rk[:, :], float(CAP), None, ALU.is_lt))
                    chain(v.scalar_tensor_tensor(slotf[:, 0, :], flat_idx, float(CAP), rk[:, :], ALU.mult, ALU.add))
                    chain(v.tensor_scalar(slotf[:, 1, :], slotf[:, 0, :], float(2 * NSLOT), None, ALU.add))
                    chain(v.scalar_tensor_tensor(slotf[:, 2, :], keep[:, :], float(-2 * NSLOT), slotf[:, 1, :],
                                                 ALU.mult, ALU.add))
                    chain(v.tensor_copy(put_at[:, :], slotf[:, 2, :]))
                    chain(v.tensor_tensor(slotf[:, 1, :], slotf[:, 0, :], keep[:, :], ALU.mult))
                    v.tensor_copy(get_at[:, :], slotf[:, 1, :]).then_inc(idx_ok, 1)
                    dve.wait_ge(ediff_ok, 1)
                    chain(v.tensor_scalar(wt[:, 2, :], wt[:, 1, :], 1.0, None, ALU.add))
                    chain(v.reciprocal(wt[:, 3, :], wt[:, 2, :]))
                    chain(v.tensor_tensor(wt[:, 4, :], wt[:, 3, :], wt[:, 1, :], ALU.mult))
                    for k in range(TOPK):
                        v.tensor_tensor(wk_[:, k, :], wt[:, 3 + k, :], keep[:, k * NT:(k + 1) * NT],
                                        ALU.mult).then_inc(wts_ok, 1)

            dve.wait_ge(scattered, 16)
            for e in range(E + 1):
                if e < E:
                    dve.wait_ge(xbt_ps, e + 1)
                    if e >= 2:
                        for i in range(2):
                            dve.wait_ge(up_full[i], (e - 1) * NF // 2)
                    v.tensor_copy(XBT[:, e % 2, 0:QB], SC[0][:, :]).then_inc(xbt_ok, 1)
                    v.tensor_copy(XBT[:, e % 2, QB:CAP], SC[1][:, 0:CAP - QB]).then_inc(xbt_ok, 1)
                if e >= 1:
                    f = e - 1
                    dve.wait_ge(down_ps, f + 1)
                    if f >= 2:
                        dve.wait_ge(yb_out[f % 2], 16 * (f // 2))
                    v.tensor_copy(YB[:, f % 2, 0:4, :], AV[0][:, :].rearrange("p (t d) -> p t d", t=4)).then_inc(dve_step, 1)
                    v.tensor_copy(YB[:, f % 2, 4, :], AV[1][:, 0:D]).then_inc(dve_step, 1)
                    n[0] += 2
                    dve.wait_ge(dve_step, n[0])
                    dve.sem_inc(yb_ok, 1)
            dve.wait_ge(wts_ok, TOPK)
            for t in range(NT):
                dve.wait_ge(gathered[t], 16 * TOPK)
                chain(v.scalar_tensor_tensor(X[:, t, :], GY[:, TOPK * t, :], wk_[:, 0, t:t + 1], X[:, t, :],
                                             ALU.mult, ALU.add))
                v.scalar_tensor_tensor(X[:, t, :], GY[:, TOPK * t + 1, :], wk_[:, 1, t:t + 1], X[:, t, :],
                                       ALU.mult, ALU.add).then_inc(out_ok, 1)

        @block.tensor
        def _(pe):
            t_ = nc.tensor

            def take(step):
                r = ring[step]
                if r >= 2:
                    pe.wait_ge(free[r % 2], r // 2)
                return WK[r % 2], full[r % 2]

            pe.wait_ge(const_ok, 1)
            for s in plan:
                kind = s[0]
                if kind == "mod":
                    w, ok = take(s)
                    pe.wait_ge(silu_ok, 1)
                    t_.matmul(w[:, 0:QB], silu_b[:, :], wm[:, 0:QB], start=True, stop=True)
                    t_.matmul(w[:, QB:6 * D], silu_b[:, :], wm[:, QB:6 * D], start=True, stop=True)
                    for i in range(2):
                        last = t_.matmul(w[:, 6 * D + i:6 * D + i + 1], wm[:, i * D:(i + 1) * D], silu_b[:, 0:1],
                                         start=True, stop=True)
                    last.then_inc(ok, 1)
                elif kind == "xt":
                    b = s[1]
                    w, ok = take(s)
                    pe.wait_ge(xn_ok, TB * (b + 1))
                    for t in range(TB):
                        last = t_.transpose(w[:, t * P:(t + 1) * P], XN[:, TB * b + t, :], ident[:, :])
                    last.then_inc(ok, 1)
                elif kind in ("q", "k"):
                    b, i = s[1], int(kind == "k")
                    w, ok = take(s)
                    r = ring[("xt", b)]
                    pe.wait_ge(free[r % 2], r // 2 + 1)
                    pe.wait_ge(rot_ok, 4)
                    t_.matmul(w[:, 0:QB], wsb[:, i, :], hT[:, QB * b:QB * (b + 1)], start=True, stop=True)
                    t_.matmul(w[:, QB:2 * QB], wsb[:, 4 + i, :], hT[:, QB * b:QB * (b + 1)], start=True,
                              stop=True).then_inc(ok, 1)
                elif kind == "v":
                    b = s[1]
                    w, ok = take(s)
                    for t in range(TB):
                        last = t_.matmul(w[:, t * P:(t + 1) * P], hT[:, (TB * b + t) * P:(TB * b + t + 1) * P],
                                         wsb[:, 2, :], start=True, stop=True)
                    last.then_inc(ok, 1)
                elif kind == "max":
                    _, u, m = s
                    b, g = units()[u]
                    j, i, k0, keys = max_pieces(u)[m]
                    h = GH * g + j
                    w, ok = take(s)
                    if m == 0 and g == 0:
                        pe.wait_ge(qk_got[b], 16 * 4)
                    rows = slice(64 * (h % 2), 64 * (h % 2) + ROWS)
                    for c0 in range(0, keys, QB):
                        nk = min(QB, keys - c0)
                        ends = k0 + c0 + nk == P * (i + 1)
                        last = t_.matmul(w[:, c0:c0 + nk], QS[rows, h // 2, i * P:(i + 1) * P],
                                         KS[rows, h // 2, k0 + c0:k0 + c0 + nk], start=True, stop=not ends)
                        if ends:
                            last = t_.matmul(w[:, c0 + nk - P:c0 + nk], identb[:, :], causal[:, :],
                                             start=False, stop=True)
                    last.then_inc(ok, 1)
                elif kind == "negmax":
                    u = s[1]
                    w, ok = take(s)
                    pe.wait_ge(nmp_ok, u + 1)
                    t_.transpose(w[0:3 * GH * TB, 0:P // 2].bitcast(bf16),
                                 nmp[:, u, :, :].rearrange("p r n -> p (r n)"), identb[:, :]).then_inc(ok, 1)
                elif kind == "scores":
                    _, u, kt = s
                    b, g = units()[u]
                    q0 = first_column(u, kt)
                    if kt == 0:
                        pe.wait_ge(m_got[u % 2], 32 * (u // 2 + 1))
                        if u == 0:
                            pe.wait_ge(ones_in, 32)
                    for j in range(GH):
                        h = GH * g + j
                        t = st.tile[u, kt, j]
                        rows = slice(64 * (h % 2), 64 * (h % 2) + KROWS)
                        if t >= 2:
                            pe.wait_ge(exped, t - 1)
                        t_.matmul(SC[t % 2][:, q0:QB], KS[rows, h // 2, kt * P:(kt + 1) * P],
                                  QS[rows, h // 2, QB * b + q0:QB * (b + 1)], start=True,
                                  stop=True).then_inc(scored, 1)
                elif kind == "av":
                    _, u, kt = s
                    b, g = units()[u]
                    q0 = first_column(u, kt)
                    pe.wait_ge(exped, st.tile[u, kt, GH - 1] + 1)
                    if (u, kt, GH - 1) in st.diag:
                        pe.wait_ge(masked, st.diag[u, kt, GH - 1])
                    if u == 0 and kt == 0:
                        pe.wait_ge(dve_const, 2)
                        r = ring[("v", NB - 1)]
                        pe.wait_ge(free[r % 2], r // 2 + 1)
                    if kt == 0 and u >= 2:
                        pe.wait_ge(evaced, u - 1)
                    for j in range(GH):
                        last = t_.matmul(AV[u % 2][32 * j:32 * j + DK + 1, q0:QB], VX[:, kt, GH * g + j, :],
                                         PRB[:, st.tile[u, kt, j] % PR, q0:QB], start=(kt == 0),
                                         stop=(kt == TB * (b + 1) - 1))
                    last.then_inc(av_ok, 1)
                elif kind == "norm":
                    _, b, h2 = s
                    w, ok = take(s)
                    pe.wait_ge(evaced, NG * (b + 1))
                    for t in range(2):
                        for g in range(NG):
                            c0 = (2 * h2 + t) * P
                            last = t_.transpose(w[:, t * QB + g * P:t * QB + (g + 1) * P], OT[:, g, c0:c0 + P],
                                                ident[:, :])
                    last.then_inc(ok, 1)
                    pe.wait_ge(ok, ring[s] // 2 + 1)
                    pe.sem_inc(norm_read, 1)
                elif kind == "ot":
                    w, ok = take(s)
                    pe.wait_ge(on_ok, 2 * (nth[s] + 1))
                    for t in range(2):
                        last = t_.transpose(w[:, t * P:(t + 1) * P], On[:, nth[s] % 2, t * D:(t + 1) * D], ident[:, :])
                    last.then_inc(ok, 1)
                elif kind == "wo":
                    w, ok = take(s)
                    r = ring[("ot",) + s[1:]]
                    pe.wait_ge(free[r % 2], r // 2 + 1)
                    pe.wait_ge(wo_ok, 1)
                    for t in range(2):
                        last = t_.matmul(w[:, t * P:(t + 1) * P], OnT[:, nth[s] % 2, t * P:(t + 1) * P],
                                         wsb[:, 3, :], start=True, stop=True)
                    last.then_inc(ok, 1)
                elif kind == "h2t":
                    b = s[1]
                    w, ok = take(s)
                    pe.wait_ge(h2_ok, b + 1)
                    for t in range(TB):
                        last = t_.transpose(w[:, t * P:(t + 1) * P], XN[:, TB * b + t, :], ident[:, :])
                    last.then_inc(ok, 1)
                elif kind == "logit":
                    b = s[1]
                    w, ok = take(s)
                    r = ring[("h2t", b)]
                    pe.wait_ge(free[r % 2], r // 2 + 1)
                    pe.wait_ge(wg_in, 16)
                    for t in range(TB):
                        last = t_.matmul(w[:, t * E:(t + 1) * E], hT[:, (TB * b + t) * P:(TB * b + t + 1) * P],
                                         wg[:, :], start=True, stop=True)
                    last.then_inc(ok, 1)
                elif kind == "rank":
                    w, ok = take(s)
                    pe.wait_ge(oh_ok, E)
                    oh = OH.rearrange("p e k t -> p (e k t)")
                    t_.matmul(w[:, 0:E * TOPK * NT], before[:, :], oh, start=True, stop=True)
                    t_.matmul(w[:, QB:QB + E * TOPK * NT], ones[:, :], oh, start=True, stop=True).then_inc(ok, 1)

            def turn(e):
                pe.wait_ge(xb_in[e % 2], 16 * (e // 2 + 1))
                if e == 0:
                    pe.wait_ge(exped, len(st.tile))
                else:
                    pe.wait_ge(xbt_ok, 2 * e)
                for t in range(CT):
                    dst = SC[0][:, t * P:(t + 1) * P] if t < 4 else SC[1][:, 0:P]
                    last = t_.transpose(dst, XB[:, e % 2, t, :], ident[:, :])
                last.then_inc(xbt_ps, 1)

            for i in range(2):
                last_use = (NRING - 1) if (NRING - 1) % 2 == i else NRING - 2
                pe.wait_ge(free[i], last_use // 2 + 1)
            pe.wait_ge(w1_in, 16)
            pe.wait_ge(w2_ok, E)
            pe.wait_ge(evaced, NU)
            turn(0)
            for e in range(E):
                pe.wait_ge(xbt_ok, 2 * (e + 1))
                for f in range(NF):
                    m = e * NF + f
                    if m >= 2:
                        pe.wait_ge(up_free[m % 2], m // 2)
                    for i in range(2):
                        last = t_.matmul(WK[m % 2][:, i * QB:i * QB + CAP // 2], W1[:, e, f * P:(f + 1) * P],
                                         XBT[:, e % 2, i * CAP // 2:(i + 1) * CAP // 2], start=True, stop=True)
                    last.then_inc(up_full[m % 2], 1)
                if e + 1 < E:
                    turn(e + 1)
                for i in range(2):
                    pe.wait_ge(up_free[i], (e + 1) * NF // 2)
                if e >= 1:
                    pe.wait_ge(yb_ok, e)
                for t in range(CT):
                    dst = AV[0][:, t * D:(t + 1) * D] if t < 4 else AV[1][:, 0:D]
                    for f in range(NF):
                        last = t_.matmul(dst, HG[:, e % 2, f, t * P:(t + 1) * P], W2[:, e, f, :],
                                         start=(f == 0), stop=(f == NF - 1))
                last.then_inc(down_ps, 1)


_INS = ["L0_attn_x", "L0_attn_Wq", "L0_attn_Wk", "L0_attn_Wv", "L0_attn_Wo", "L0_ffn_w_g", "L0_ffn_c_fc",
        "L0_ffn_c_proj", "L0_c", "L0_wmod"]


def rotary_tables():
    inv = (1.0 / np.float32(10000.0) ** (np.arange(0, DK, 2, dtype=np.float32) / np.float32(DK))).astype(np.float32)
    ang = np.outer(np.arange(S, dtype=np.float32), inv).astype(np.float32)
    cos, sin = (np.repeat(f(ang).astype(np.float32), 2, axis=-1).T for f in (np.cos, np.sin))
    return np.ascontiguousarray(np.tile(cos, (H, 1))), np.ascontiguousarray(np.tile(sin, (H, 1)))


def kernel(**inputs):
    import concourse.bacc as _bacc
    from concourse import mybir as _mybir
    from concourse.bass_utils import run_bass_kernel_spmd as _run

    nc = _bacc.Bacc("TRN2", target_bir_lowering=False, num_devices=1)
    arrays, args = {}, []
    for name in _INS:
        arrays[f"in_{name}_dram"] = np.ascontiguousarray(inputs[name])
    arrays["rope_cos"], arrays["rope_sin"] = rotary_tables()
    import ml_dtypes
    arrays["ones_rows"] = np.ones((3, NPAIR * S), ml_dtypes.bfloat16)
    for name, a in arrays.items():
        args.append(nc.dram_tensor(name, a.shape, _mybir.dt.from_np(a.dtype), kind="ExternalInput").ap())
    args.append(nc.dram_tensor("out_dram", (1, S, D), _mybir.dt.float32, kind="ExternalOutput").ap())
    block_kernel(nc, *args)
    r = _run(nc, [arrays], core_ids=[0])
    return r.results[0]["out_dram"]
```

```python
import numpy as np
import concourse.bass as bass
from concourse import mybir
from contextlib import ExitStack

P = 128
S = 2048
D = 128
H = 16
DK = D // H
NT = S // P
QB = 512
NB = S // QB
TB = QB // P
GH = 4
NG = H // GH
NU = NB * NG
NPAIR = H // 2
E = 8
TOPK = 2
F = 4 * D
NF = F // P
CAP = 2 * int(1.25 * S) // E
CT = CAP // P
NSLOT = E * CAP
SCALE = float(DK) ** -0.5
EPS = 1e-5

TERMS = [(0, 0), (0, 1), (1, 0), (1, 1), (0, 2), (2, 0)]
ROWS = DK * len(TERMS)
KROWS = ROWS + 3
MW = 1024
PR = 16
AVLAG = 2


def units():
    return [(b, g) for b in range(NB) for g in range(NG)]


def max_pieces(u):
    b, _ = units()[u]
    return [(j, i, k0, min(MW, P * (i + 1) - k0))
            for j in range(GH) for i in range(TB * b, TB * (b + 1)) for k0 in range(0, P * (i + 1), MW)]


EPILOGUE = ["norm", "ot", "wo"]


def make_plan():
    plan = [("mod", 0)] + [("xt", b) for b in range(NB)] + [("q", 0), ("k", 0), ("v", 0), ("q", 1), ("k", 1)]
    pieces = [(u, n, c) for u in range(NU) for n, p in enumerate(max_pieces(u)) for c in range(-(-p[3] // QB))]
    at = 0
    done = 0.0
    later = []

    def cost(u, n, c):
        return min(QB, max_pieces(u)[n][3] - QB * c) + 40

    def put_off(ticks, step):
        later.append([ticks, step])
        later.sort(key=lambda x: x[0])

    def tick():
        for x in later:
            x[0] -= 1
        if later and later[0][0] <= 0 and (at == len(pieces) or pieces[at][2] == 0):
            plan.append(later.pop(0)[1])

    def piece():
        nonlocal at, done
        u, n, c = pieces[at]
        plan.append(("max2" if c else "max", u, n))
        done += cost(*pieces[at])
        at += 1
        if at == len(pieces) or pieces[at][0] > u:
            plan.append(("maxend", u))
            put_off(6, ("negmax", u))
        tick()

    def flush(step):
        while pieces[at - 1][1] == pieces[min(at, len(pieces) - 1)][1] and at < len(pieces) and pieces[at][2]:
            piece()
        while step not in plan:
            plan.append(later.pop(0)[1])

    cum_m, cum_s = [0], [0]
    for u, (b, _) in enumerate(units()):
        cum_m.append(cum_m[-1] + sum(cost(*p) for p in pieces if p[0] == u))
        cum_s.append(cum_s[-1] + GH * sum(QB - first_column(u, kt) for kt in range(TB * (b + 1))))
    for n, step in enumerate([("v", 1), ("q", 2), ("k", 2), ("v", 2), ("q", 3), ("k", 3), ("v", 3)]):
        put_off(8 + 8 * n, step)
    while pieces[at][0] == 0:
        piece()
    avs = []
    for u, (b, g) in enumerate(units()):
        while pieces[min(at, len(pieces) - 1)][0] <= u and at < len(pieces):
            piece()
        while ("negmax", u) not in plan:
            if at < len(pieces) and (pieces[at][0] <= u + 1 or pieces[at][2]):
                piece()
            else:
                plan.append(later.pop(0)[1])
        rate, base, went = 0.0, done, 0
        for v in range(u + 1, NU):
            due = max(cum_s[v] - 6000, cum_s[u] + (cum_s[u + 1] - cum_s[u]) * 0.6)
            rate = max(rate, (cum_m[v + 1] - done) / (due - cum_s[u]))
        for kt in range(TB * (b + 1)):
            for j in range(GH):
                plan.append(("score", u, kt, j))
                went += QB - first_column(u, kt)
                tick()
                while at < len(pieces) and done < base + rate * went:
                    piece()
            avs.append((u, kt))
            while len(avs) > AVLAG + (avs[0][1] == 0):
                uu, kk = avs.pop(0)
                plan.append(("av", uu, kk))
                if kk == TB * (units()[uu][0] + 1) - 1:
                    plan.append(("evac", uu))
                    if uu % NG == NG - 1:
                        n = 0
                        for kind in EPILOGUE:
                            for half in range(2):
                                put_off(6 + 8 * n, (kind, uu // NG, half))
                                n += 1
                        for kind in ("h2t", "logit"):
                            put_off(12 + 8 * n, (kind, uu // NG))
                            n += 2
    plan += [("av", uu, kk) for uu, kk in avs] + [("evac", NU - 1)] + [x[1] for x in later]
    plan += [(kind, NB - 1, half) for kind in EPILOGUE for half in range(2)]
    plan += [("h2t", NB - 1), ("logit", NB - 1), ("rank", 0)]
    return plan


def first_column(u, kt):
    return P * max(0, kt - TB * units()[u][0])


class Steps:

    def __init__(self):
        self.plan = make_plan()
        ringless = ("score", "av", "evac", "maxend", "max2")
        self.ring = {s: n for n, s in enumerate(x for x in self.plan if x[0] not in ringless)}
        self.nth = {}
        count = {}
        for s in self.plan:
            self.nth[s] = count.get(s[0], 0)
            count[s[0]] = self.nth[s] + 1
        self.tile = {}
        for s in self.plan:
            if s[0] == "score":
                self.tile[s[1:]] = len(self.tile)
        self.diag = {}
        for s in self.plan:
            if s[0] == "score" and s[2] >= TB * units()[s[1]][0]:
                self.diag[s[1:]] = len(self.diag) + 1


def block_kernel(nc, x, Wq, Wk, Wv, Wo, w_g, c_fc, c_proj, c, wmod, cos_t, sin_t, pad_t, out):
    f32, bf16, u32 = mybir.dt.float32, mybir.dt.bfloat16, mybir.dt.uint32
    ALU, ACT, AX = mybir.AluOpType, mybir.ActivationFunctionType, mybir.AxisListType
    st = Steps()
    plan, ring, nth = st.plan, st.ring, st.nth
    NRING = len(ring)

    q_rows = nc.dram_tensor("q_rows", (H, ROWS, S), bf16)
    k_rows = nc.dram_tensor("k_rows", (H, ROWS, S), bf16)
    m_rows = nc.dram_tensor("m_rows", (NU, 3 * TB * GH, P), bf16)
    slots_x = nc.dram_tensor("slots_x", (NSLOT, D), f32)
    slots_y = nc.dram_tensor("slots_y", (NSLOT, D), f32)

    ctx = ExitStack()
    with ctx:
        def sb(name, shape, dt=f32):
            return ctx.enter_context(nc.sbuf_tensor(name, shape, dt))

        def sem(name):
            return ctx.enter_context(nc.semaphore(name))

        X = sb("X", [P, NT, D])
        XN = sb("XN", [P, NT, D])
        hT = sb("hT", [P, S])
        KS = sb("KS", [P, NPAIR, S], bf16)
        QP = sb("QP", [P, 2, NPAIR, 2, QB], bf16)
        VX = sb("VX", [P, NT, H, DK + 1])
        PRB = sb("PRB", [P, PR, QB])
        part_set = sb("part_set", [P, 2, 2, 3, QB], bf16)
        CS = sb("CS", [P, 2, S])
        W1 = CS[:, :, :].rearrange("p a s -> p (a s)").rearrange("p (e f) -> p e f", e=E)
        W2 = sb("W2", [P, E, NF, D])
        OT = sb("OT", [P, NG, QB])
        RT = sb("RT", [P, 2, 3, QB])
        wsb = sb("wsb", [P, 6, D])
        wg = sb("wg", [P, E])
        wm = RT[:, :, :, :].rearrange("p a b n -> p (a b n)")[:, 0:6 * D]
        MODB = sb("MODB", [P, 6, D])
        modT = sb("modT", [P, 2])
        ccol = sb("ccol", [P, 4])
        silu_b = sb("silu_b", [P, P])
        stats = sb("stats", [P, NT, 6])
        mv = sb("mv", [P, 2, NT, 2])
        veps = sb("veps", [P, NT])
        half = sb("half", [P, NT])
        rstd = sb("rstd", [P, 2, NT])
        ident = sb("ident", [P, P])
        identb = sb("identb", [P, P], bf16)
        causal = sb("causal", [P, P], bf16)
        before = sb("before", [P, P])
        ones = sb("ones", [P, P])
        mpart = sb("mpart", [P, 2, 2, GH * TB])
        mx = sb("mx", [P, 2, GH * TB])
        nm = sb("nm", [P, 2, 3, GH * TB])
        nmp = sb("nmp", [P, 2, 3, GH * TB], bf16)
        mrow = sb("mrow", [3 * GH * TB, 2, P], bf16)
        rl = sb("rl", [P, 2, H])
        LG = sb("LG", [P, NT, E])
        T8 = sb("T8", [P, NT, 8])
        I8 = sb("I8", [P, NT, 8], u32)
        idxf = sb("idxf", [P, TOPK, NT])
        io = sb("io", [P, E])
        tables = part_set[:, :, :, :, :].rearrange("p a b r n -> p (a b r n)").bitcast(f32)[:, 0:3 * E * TOPK * NT].rearrange("p (a e n) -> p a e n", a=3, e=E)
        OH = tables[:, 0].rearrange("p e (k t) -> p e k t", k=TOPK)
        incl, restart = tables[:, 1], tables[:, 2]
        rk = sb("rk", [P, TOPK * NT])
        keep = sb("keep", [P, TOPK * NT])
        slotf = sb("slotf", [P, 3, TOPK * NT])
        put_at = sb("put_at", [P, TOPK * NT], u32)
        get_at = sb("get_at", [P, TOPK * NT], u32)
        wt = sb("wt", [P, 5, NT])
        wk_ = sb("wk_", [P, TOPK, NT])
        rt_flat = RT[:, :, :, :].rearrange("p a b n -> p (a b n)")
        zeros = rt_flat[:, 0:CAP]
        On = rt_flat[:, 2 * QB:3 * QB].rearrange("p (n d) -> p n d", n=2)
        OnT = rt_flat[:, 3 * QB:4 * QB].rearrange("p (n d) -> p n d", n=2)
        flat = KS[:, :, :].rearrange("p a s -> p (a s)").bitcast(f32)
        XB = flat[:, 0:2 * CAP].rearrange("p (n t d) -> p n t d", n=2, t=CT)
        XBT = flat[:, 2 * CAP:4 * CAP].rearrange("p (n s) -> p n s", n=2)
        YB = flat[:, 4 * CAP:6 * CAP].rearrange("p (n t d) -> p n t d", n=2, t=CT)
        flatq = QP[:, :, :, :, :].rearrange("p c h a s -> p (c h a s)").bitcast(f32)
        HG = flatq[:, 0:2 * NF * CAP].rearrange("p (n f s) -> p n f s", n=2, f=NF)
        GY = PRB[:, :, :].rearrange("p a b -> p (a b)")[:, 0:TOPK * NT * D].rearrange("p (n d) -> p n d", d=D)

        WK = [ctx.enter_context(nc.psum_tensor(f"work{i}", [P, 2 * QB], f32)) for i in range(2)]
        SC = [ctx.enter_context(nc.psum_tensor(f"score{i}", [P, QB], f32)) for i in range(3)]
        AV = ctx.enter_context(nc.psum_tensor("av", [P, QB], f32))

        qp_zero = sem("qp_zero")
        w_in, mod_in, rope_in, ones_in, w2_in, w1_in = (
            sem(n) for n in ("w_in", "mod_in", "rope_in", "ones_in", "w2_in", "w1_in"))
        x_in = [sem(f"x_in{b}") for b in range(NB)]
        wg_in, zero_out = sem("wg_in"), sem("zero_out")
        qk_put = [sem(f"qk_put{b}") for b in range(NB)]
        qk_got = [sem(f"qk_got{b}") for b in range(NB)]
        m_put, m_got = [sem(f"m_put{i}") for i in range(2)], [sem(f"m_got{i}") for i in range(2)]
        const_ok = sem("const_ok")
        pool_step = sem("pool_step")
        dve_step = sem("dve_step")
        dve_const = sem("dve_const")
        act_silu = sem("act_silu")
        silu_ok = sem("silu_ok")
        rot_ok = sem("rot_ok")
        stats_ok, rstd_ok, xn_ok = sem("stats_ok"), sem("rstd_ok"), sem("xn_ok")
        modt_ok, modb_ok = sem("modt_ok"), sem("modb_ok")
        full = [sem(f"full{i}") for i in range(2)]
        free = [sem(f"free{i}") for i in range(2)]
        ht_ok, vx_ok, roped, kparts_ok, qparts_ok = (
            sem(n) for n in ("ht_ok", "vx_ok", "roped", "kparts_ok", "qparts_ok"))
        max_ok, mx_ok, nmp_ok, mrow_ok = sem("max_ok"), sem("mx_ok"), sem("nmp_ok"), sem("mrow_ok")
        scored, exped, masked, av_ok, evaced = (
            sem(n) for n in ("scored", "exped", "masked", "av_ok", "evaced"))
        on_ok, ont_ok, x2_ok, stats2_ok, xn2_ok, h2_ok, h2t_ok, logit_ok = (
            sem(n) for n in ("on_ok", "ont_ok", "x2_ok", "stats2_ok", "xn2_ok", "h2_ok", "h2t_ok", "logit_ok"))
        norm_read, h2t_read = sem("norm_read"), sem("h2t_read")
        wo_ok, w2_ok = sem("wo_ok"), sem("w2_ok")
        top_ok, diff_ok, ediff_ok, oh_ok, idx_ok, wts_ok = (
            sem(n) for n in ("top_ok", "diff_ok", "ediff_ok", "oh_ok", "idx_ok", "wts_ok"))
        scattered, restart_ok = sem("scattered"), sem("restart_ok")
        xb_in = [sem(f"xb_in{i}") for i in range(2)]
        xbt_ps, xbt_ok = sem("xbt_ps"), sem("xbt_ok")
        up_full, up_free = [sem(f"up_full{i}") for i in range(2)], [sem(f"up_free{i}") for i in range(2)]
        down_ps, yb_ok = sem("down_ps"), sem("yb_ok")
        yb_out = [sem(f"yb_out{i}") for i in range(2)]
        gathered = [sem(f"gathered{i}") for i in range(NT)]
        sum_ok, out_ok, out_done = sem("sum_ok"), sem("out_ok"), sem("out_done")

        block = ctx.enter_context(nc.Block())

        def wait_full(eng, step):
            eng.wait_ge(full[ring[step] % 2], ring[step] // 2 + 1)
            return WK[ring[step] % 2]

        def parts(which, b, r):
            return part_set[:, which, b % 2, r, :]

        def prev(s):
            return (s[1] - 1, s[2])

        def release(eng, s):
            eng.sem_inc(free[ring[s] % 2], 1)

        sign = RT[:, 0, 0, 0:D]

        q_pairs = q_rows.ap().rearrange("(a b) r s -> b r a s", b=2)
        k_pairs = k_rows.ap().rearrange("(a b) r s -> b r a s", b=2)

        @block.sync
        def _(sp):
            x_t = x[0].rearrange("(t p) d -> p t d", p=P)
            for b in range(NB):
                sp.dma_start(X[:, TB * b:TB * (b + 1), :], x_t[:, TB * b:TB * (b + 1), :]).then_inc(x_in[b], 16)
                if b == 0:
                    sp.dma_start(ccol[:, 0:1], c.rearrange("a p -> p a")).then_inc(mod_in, 16)
                    sp.dma_start(wm[:, :], wmod).then_inc(mod_in, 16)
            for n, w in enumerate((Wq, Wk, Wv, Wo)):
                sp.dma_start(wsb[:, n, :], w).then_inc(w_in, 16)
            sp.dma_start(CS[:, 0, :], cos_t).then_inc(rope_in, 16)
            sp.dma_start(CS[:, 1, :], sin_t).then_inc(rope_in, 16)
            for par in range(2):
                sp.dma_start(KS[64 * par + ROWS:64 * (par + 1), :, :],
                             pad_t.rearrange("r (a s) -> r a s", a=NPAIR)).then_inc(ones_in, 16)
            sp.dma_start(wg[:, :], w_g).then_inc(wg_in, 16)

            def expand(b):
                cols = slice(QB * b, QB * (b + 1))
                sp.wait_ge(qparts_ok, b + 1)
                for t, (a, _) in enumerate(TERMS):
                    sp.dma_start(q_rows[:, DK * t:DK * (t + 1), cols], parts(0, b, a)).then_inc(qk_put[b], 16)
                sp.wait_ge(kparts_ok, b + 1)
                for t, (_, a) in enumerate(TERMS):
                    sp.dma_start(k_rows[:, DK * t:DK * (t + 1), cols], parts(1, b, a)).then_inc(qk_put[b], 16)
                sp.wait_ge(qk_put[b], 16 * 2 * len(TERMS))
                for par in range(2):
                    sp.dma_start(KS[64 * par:64 * par + ROWS, :, cols],
                                 k_pairs[par, :, :, cols]).then_inc(qk_got[b], 16)
                if b < 2:
                    sp.wait_ge(qp_zero, 2 * (b + 1))
                    for par in range(2):
                        sp.dma_start(QP[64 * par:64 * par + ROWS, par, :, b, :],
                                     q_pairs[par, :, :, cols]).then_inc(qk_got[b], 16)

            def put_negmax(u):
                b, g = units()[u]
                sp.wait_ge(mrow_ok, u + 1)
                sp.dma_start(m_rows[u], mrow[:, u % 2, :]).then_inc(m_put[u % 2], 16)
                sp.wait_ge(m_put[u % 2], 16 * (u // 2 + 1))
                src = m_rows[u].rearrange("(r a b i) q -> b r a (i q)", r=3, a=2, b=2)
                for par in range(2):
                    sp.dma_start(QP[64 * par + ROWS:64 * par + KROWS, par, 2 * g:2 * g + 2, b % 2, :],
                                 src[par]).then_inc(m_got[u % 2], 16)

            expand(0)
            expand(1)
            put_negmax(0)
            expand(2)
            put_negmax(1)
            expand(3)
            sp.dma_start(W2[:, :, :, :], c_proj.rearrange("e (f p) d -> p e f d", p=P)).then_inc(w2_in, 16)
            put_negmax(2)
            sp.wait_ge(roped, 2 * NB)
            sp.dma_start(W1, c_fc.rearrange("e d f -> d e f")).then_inc(w1_in, 16)
            put_negmax(3)
            sp.wait_ge(dve_const, 2)
            for e in range(E):
                sp.dma_start(slots_x[e * CAP:(e + 1) * CAP, :].rearrange("(p t) d -> p (t d)", p=P),
                             zeros).then_inc(zero_out, 16)
            for u in range(4, NU):
                put_negmax(u)

            sp.wait_ge(scattered, 16 * TOPK * NT)
            for e in range(E + 1):
                if e < E:
                    if e >= 2:
                        sp.wait_ge(xbt_ps, e - 1)
                    sp.dma_start(XB[:, e % 2], slots_x[e * CAP:(e + 1) * CAP, :]
                                 .rearrange("(t p) d -> p t d", p=P)).then_inc(xb_in[e % 2], 16)
                if e >= 1:
                    sp.wait_ge(yb_ok, e)
                    sp.dma_start(slots_y[(e - 1) * CAP:e * CAP, :].rearrange("(t p) d -> p t d", p=P),
                                 YB[:, (e - 1) % 2]).then_inc(yb_out[(e - 1) % 2], 16)
            out_t = out[0].rearrange("(t p) d -> p t d", p=P)
            for b in range(NB):
                sp.wait_ge(out_ok, TB * (b + 1))
                sp.dma_start(out_t[:, TB * b:TB * (b + 1), :], X[:, TB * b:TB * (b + 1), :]).then_inc(out_done, 16)
            sp.wait_ge(out_done, 16 * NB)

        @block.gpsimd
        def _(pool):
            g = nc.gpsimd
            n = [0]

            def chain(ins):
                n[0] += 1
                ins.then_inc(pool_step, 1)
                pool.wait_ge(pool_step, n[0])

            for w in range(2):
                g.memset(QP[:, 1, :, w, :].bitcast(f32), 0.0).then_inc(qp_zero, 1)
            g.memset(half[:, :], -0.5).then_inc(pool_step, 1)
            g.memset(ones[:, :], 1.0).then_inc(pool_step, 1)
            g.memset(ident[:, :], 0.0).then_inc(pool_step, 1)
            g.memset(identb[:, :], 0.0).then_inc(pool_step, 1)
            g.memset(causal[:, :], 0.0).then_inc(pool_step, 1)
            n[0] = 5
            pool.wait_ge(pool_step, n[0])
            for m in (ident, identb):
                g.affine_select(out=m[:, :], in_=m[:, :], compare_op=ALU.not_equal, fill=1.0, base=0,
                                pattern=[[-1, P]], channel_multiplier=1).then_inc(pool_step, 1)
            g.affine_select(out=causal[:, :], in_=causal[:, :], compare_op=ALU.is_ge, fill=-1e30, base=0,
                            pattern=[[-1, P]], channel_multiplier=1).then_inc(pool_step, 1)
            g.affine_select(out=before[:, :], in_=ones[:, :], compare_op=ALU.is_gt, fill=0.0, base=0,
                            pattern=[[1, P]], channel_multiplier=-1).then_inc(pool_step, 1)
            g.memset(VX[:, :, :, DK:DK + 1], 1.0).then_inc(pool_step, 1)
            n[0] += 5
            chain(g.iota(I8[:, 0, :], pattern=[[1, E]], base=0, channel_multiplier=0))
            chain(g.tensor_copy(io[:, :], I8[:, 0, :]))
            pool.sem_inc(const_ok, 1)

            def rstd_of(which, tiles):
                chain(g.tensor_scalar(veps[:, tiles], mv[:, which, tiles, 1], EPS, None, ALU.add))
                g.tensor_tensor(rstd[:, which, tiles], veps[:, tiles], half[:, tiles], ALU.pow).then_inc(rstd_ok, 1)

            for b in range(NB):
                pool.wait_ge(stats_ok, b + 1)
                rstd_of(0, slice(TB * b, TB * (b + 1)))
            gates = 0
            for s in plan:
                if s[0] == "k":
                    b = s[1]
                    pool.wait_ge(roped, 2 * b + 2)
                    if b >= 2:
                        pool.wait_ge(qk_put[b - 2], 16 * 2 * len(TERMS))
                    r, d1 = RT[:, 1, 2, :], RT[:, 1, 0, :]
                    chain(g.tensor_scalar(parts(1, b, 0), r, 1.0, 1.0, ALU.mult, ALU.mult))
                    chain(g.tensor_tensor(d1, r, parts(1, b, 0), ALU.subtract))
                    chain(g.tensor_scalar(parts(1, b, 1), d1, 1.0, 1.0, ALU.mult, ALU.mult))
                    chain(g.tensor_tensor(r, d1, parts(1, b, 1), ALU.subtract))
                    g.tensor_scalar(parts(1, b, 2), r, 1.0, 1.0, ALU.mult, ALU.mult).then_inc(kparts_ok, 1)
                elif s[0] == "maxend":
                    u = s[1]
                    pool.wait_ge(mx_ok, u + 1)
                    if u >= 2:
                        pool.wait_ge(mrow_ok, u - 1)
                    chain(g.tensor_scalar(nm[:, u % 2, 0, :], mx[:, u % 2, :], -1.0, 1.0, ALU.mult, ALU.mult))
                    chain(g.tensor_copy(nmp[:, u % 2, 0, :], nm[:, u % 2, 0, :]))
                    chain(g.tensor_tensor(nm[:, u % 2, 1, :], nm[:, u % 2, 0, :], nmp[:, u % 2, 0, :], ALU.subtract))
                    chain(g.tensor_copy(nmp[:, u % 2, 1, :], nm[:, u % 2, 1, :]))
                    chain(g.tensor_tensor(nm[:, u % 2, 2, :], nm[:, u % 2, 1, :], nmp[:, u % 2, 1, :], ALU.subtract))
                    g.tensor_copy(nmp[:, u % 2, 2, :], nm[:, u % 2, 2, :]).then_inc(nmp_ok, 1)
                elif s[0] == "score":
                    _, u, kt, j = s
                    if kt >= TB * units()[u][0]:
                        t = st.tile[u, kt, j]
                        pool.wait_ge(exped, t + 1)
                        tile = PRB[:, t % PR, first_column(u, kt):first_column(u, kt) + P]
                        g.affine_select(out=tile, in_=tile, compare_op=ALU.is_ge, fill=0.0, base=0,
                                        pattern=[[1, P]], channel_multiplier=-1).then_inc(masked, 1)
                    elif u >= NG and gates < E:
                        if gates == 0:
                            pool.wait_ge(modb_ok, 1)
                            pool.wait_ge(w_in, 16 * 4)
                            g.tensor_tensor(wsb[:, 3, :], wsb[:, 3, :], MODB[:, 2, :], ALU.mult).then_inc(wo_ok, 1)
                            pool.wait_ge(w2_in, 16)
                        g.tensor_tensor(W2[:, gates], W2[:, gates],
                                        MODB[:, 5:6, :].to_broadcast([P, NF, D]), ALU.mult).then_inc(w2_ok, 1)
                        gates += 1
                elif s[0] == "h2t":
                    b = s[1]
                    tiles = slice(TB * b, TB * (b + 1))
                    if b == 0:
                        pool.wait_ge(qk_put[NB - 1], 16 * 2 * len(TERMS))
                        chain(g.memset(restart, 1.0))
                        g.memset(restart[:, :, 0:1], 0.0).then_inc(restart_ok, 1)
                    pool.wait_ge(stats2_ok, b + 1)
                    rstd_of(1, tiles)
                    pool.wait_ge(xn2_ok, b + 1)
                    chain(g.tensor_tensor(XN[:, tiles, :], XN[:, tiles, :],
                                          MODB[:, 4:5, :].to_broadcast([P, TB, D]), ALU.mult))
                    g.tensor_tensor(XN[:, tiles, :], XN[:, tiles, :],
                                    MODB[:, 3:4, :].to_broadcast([P, TB, D]), ALU.add).then_inc(h2_ok, 1)
            pool.wait_ge(idx_ok, 1)
            pool.wait_ge(h2_ok, NB)
            pool.wait_ge(zero_out, 16 * E)
            for k in range(TOPK):
                for t in range(NT):
                    m = k * NT + t
                    g.indirect_dma_start(out=slots_x[:, :],
                                         out_offset=bass.IndirectOffsetOnAxis(ap=put_at[:, m:m + 1], axis=0),
                                         in_=XN[:, t, :], in_offset=None, bounds_check=NSLOT - 1,
                                         oob_is_err=False).then_inc(scattered, 16)
            for i in range(2):
                pool.wait_ge(yb_out[i], 16 * E // 2)
            for t in range(NT):
                for k in range(TOPK):
                    m = k * NT + t
                    g.indirect_dma_start(out=GY[:, TOPK * t + k, :], out_offset=None, in_=slots_y[:, :],
                                         in_offset=bass.IndirectOffsetOnAxis(ap=get_at[:, m:m + 1], axis=0),
                                         bounds_check=NSLOT - 1, oob_is_err=False).then_inc(gathered[t], 16)

        @block.scalar
        def _(act):
            a = nc.scalar
            act.wait_ge(mod_in, 32)
            a.activation(ccol[:, 1:2], ccol[:, 0:1], ACT.Exp, scale=-1.0).then_inc(act_silu, 1)
            for s in plan:
                if s[0] == "xt":
                    b = s[1]
                    w = wait_full(act, s)
                    act.wait_ge(modt_ok, 2)
                    a.activation(hT[:, QB * b:QB * (b + 1)], w[:, 0:QB], ACT.Identity, bias=modT[:, 0:1],
                                 scale=modT[:, 1:2]).then_inc(free[ring[s] % 2], 1)
                elif s[0] == "v":
                    b = s[1]
                    w = wait_full(act, s)
                    act.wait_ge(const_ok, 1)
                    a.activation(VX[:, TB * b:TB * (b + 1), :, 0:DK],
                                 w[:, 0:QB].rearrange("p (t h d) -> p t h d", t=TB, h=H),
                                 ACT.Copy).then_inc(free[ring[s] % 2], 1)
                elif s[0] == "negmax":
                    u = s[1]
                    w = wait_full(act, s)
                    if u >= 2:
                        act.wait_ge(m_put[u % 2], 16 * (u // 2))
                    a.activation(mrow[:, u % 2, :], w[0:3 * GH * TB, 0:P // 2].bitcast(bf16),
                                 ACT.Copy).then_inc(free[ring[s] % 2], 1)
                    act.wait_ge(free[ring[s] % 2], ring[s] // 2 + 1)
                    act.sem_inc(mrow_ok, 1)
                elif s[0] == "score":
                    _, u, kt, j = s
                    q0 = first_column(u, kt)
                    t = st.tile[u, kt, j]
                    if t >= PR:
                        act.wait_ge(av_ok, (t - PR) // GH + 1)
                    act.wait_ge(scored, t + 1)
                    a.activation(PRB[:, t % PR, q0:QB], SC[t % 3][:, q0:QB], ACT.Exp, scale=SCALE).then_inc(exped, 1)
                    b = units()[u][0] + 2
                    if u % NG == NG - 1 and kt == TB * (b - 1) - 1 and j == GH - 1 and b < NB:
                        act.wait_ge(qk_put[b], 16 * 2 * len(TERMS))
                        for par in range(2):
                            act.dma_start(QP[64 * par:64 * par + ROWS, par, :, b % 2, :],
                                          q_pairs[par, :, :, QB * b:QB * (b + 1)]).then_inc(qk_got[b], 16)
                            act.dma_start(QP[64 * par + ROWS:64 * par + KROWS, par, :, b % 2, :],
                                          pad_t[3:6, 0:NPAIR * QB].rearrange("r (a s) -> r a s", a=NPAIR))\
                               .then_inc(qk_got[b], 16)
                elif s[0] == "evac":
                    u = s[1]
                    b, g = units()[u]
                    act.wait_ge(av_ok, sum(TB * (bb + 1) for bb, _ in units()[:u + 1]))
                    if b >= 1:
                        act.wait_ge(norm_read, 2 * b)
                    a.activation(OT[:, g, :], AV[:, :], ACT.Copy).then_inc(evaced, 1)
                elif s[0] == "ot":
                    w = wait_full(act, s)
                    if nth[s] >= 2:
                        act.wait_ge(full[ring[("wo",) + prev(s)] % 2], ring[("wo",) + prev(s)] // 2 + 1)
                    a.activation(OnT[:, nth[s] % 2, :], w[:, 0:2 * P], ACT.Copy).then_inc(free[ring[s] % 2], 1)
                elif s[0] == "h2t":
                    w = wait_full(act, s)
                    a.activation(hT[:, QB * s[1]:QB * (s[1] + 1)], w[:, 0:QB], ACT.Copy).then_inc(free[ring[s] % 2], 1)
            act.wait_ge(diff_ok, 1)
            a.activation(wt[:, 1, :], wt[:, 0, :], ACT.Exp).then_inc(ediff_ok, 1)
            for e in range(E):
                for f in range(NF):
                    m = e * NF + f
                    act.wait_ge(up_full[m % 2], m // 2 + 1)
                    if e >= 2 and f == 0:
                        act.wait_ge(down_ps, e - 1)
                    a.activation(HG[:, e % 2, f, :].rearrange("p (n s) -> p n s", n=2),
                                 WK[m % 2][:, :].rearrange("p (n s) -> p n s", n=2)[:, :, 0:CAP // 2],
                                 ACT.Gelu).then_inc(up_free[m % 2], 1)

        @block.vector
        def _(dve):
            v = nc.vector
            n = [0]

            def chain(ins):
                n[0] += 1
                ins.then_inc(dve_step, 1)
                dve.wait_ge(dve_step, n[0])

            v.memset(AV[:, :], 0.0).then_inc(dve_const, 1)
            for w in range(2):
                v.memset(QP[:, 0, :, w, :].bitcast(f32), 0.0).then_inc(qp_zero, 1)
            for b in range(NB):
                dve.wait_ge(x_in[b], 16)
                for t in range(TB * b, TB * (b + 1)):
                    v.bn_stats(stats[:, t, :], X[:, t, :]).then_inc(dve_step, 1)
                n[0] += TB
                dve.wait_ge(dve_step, n[0])
                for t in range(TB * b, TB * (b + 1)):
                    v.bn_aggr(mv[:, 0, t, :], stats[:, t, :]).then_inc(dve_step, 1)
                n[0] += TB
                dve.wait_ge(dve_step, n[0])
                dve.sem_inc(stats_ok, 1)
            dve.wait_ge(act_silu, 1)
            chain(v.tensor_scalar(ccol[:, 2:3], ccol[:, 1:2], 1.0, None, ALU.add))
            chain(v.reciprocal(ccol[:, 3:4], ccol[:, 2:3]))
            chain(v.tensor_tensor(ccol[:, 1:2], ccol[:, 0:1], ccol[:, 3:4], ALU.mult))
            v.tensor_copy(silu_b[:, :], ccol[:, 1:2].to_broadcast([P, P])).then_inc(silu_ok, 1)
            for t in range(NT):
                if t % TB == 0:
                    dve.wait_ge(rstd_ok, t // TB + 1)
                v.tensor_scalar(XN[:, t, :], X[:, t, :], mv[:, 0, t, 0:1], rstd[:, 0, t:t + 1],
                                ALU.subtract, ALU.mult).then_inc(xn_ok, 1)
            dve.wait_ge(w_in, 16 * 4)
            for i in range(2):
                src = wsb[:, i, :].rearrange("p (n two) -> p n two", two=2)
                dst = wsb[:, 4 + i, :].rearrange("p (n two) -> p n two", two=2)
                v.tensor_scalar(dst[:, :, 0], src[:, :, 1], -1.0, None, ALU.mult).then_inc(rot_ok, 1)
                v.tensor_copy(dst[:, :, 1], src[:, :, 0]).then_inc(rot_ok, 1)

            for s in plan:
                kind = s[0]
                if kind == "mod":
                    w = wait_full(dve, s)
                    v.tensor_copy(modT[:, 0:1], w[:, 6 * D:6 * D + 1]).then_inc(modt_ok, 1)
                    v.tensor_scalar(modT[:, 1:2], w[:, 6 * D + 1:6 * D + 2], 1.0, None, ALU.add).then_inc(modt_ok, 1)
                    chain(v.tensor_copy(MODB[:, :, :].rearrange("p a d -> p (a d)"), w[:, 0:6 * D]))
                    for i in (2, 5):
                        chain(v.tensor_scalar(sign, MODB[:, i, :], 0.0, 2.0, ALU.is_ge, ALU.mult))
                        chain(v.tensor_scalar(sign, sign, -1.0, None, ALU.add))
                        chain(v.tensor_tensor(MODB[:, i, :], MODB[:, i, :], sign, ALU.mult))
                        chain(v.tensor_scalar(MODB[:, i, :], MODB[:, i, :], 0.25, None, ALU.max))
                        chain(v.tensor_tensor(MODB[:, i, :], MODB[:, i, :], sign, ALU.mult))
                    chain(v.tensor_scalar(MODB[:, 4, :], MODB[:, 4, :], 1.0, None, ALU.add))
                    dve.sem_inc(modb_ok, 1)
                    release(dve, s)
                elif kind in ("q", "k"):
                    b, i = s[1], kind == "k"
                    w = wait_full(dve, s)
                    dve.wait_ge(rope_in, 32)
                    if i and b:
                        dve.wait_ge(kparts_ok, b)
                    cols = slice(QB * b, QB * (b + 1))
                    v.tensor_tensor(RT[:, i, 0, :], w[:, 0:QB], CS[:, 0, cols], ALU.mult).then_inc(dve_step, 1)
                    n[0] += 1
                    chain(v.tensor_tensor(RT[:, i, 1, :], w[:, QB:2 * QB], CS[:, 1, cols], ALU.mult))
                    release(dve, s)
                    r, d1 = RT[:, i, 2, :], RT[:, i, 0, :]
                    v.tensor_tensor(r, RT[:, i, 0, :], RT[:, i, 1, :], ALU.add).then_inc(roped, 1)
                    if not i:
                        dve.wait_ge(roped, 2 * b + 1)
                        if b >= 2:
                            dve.wait_ge(qk_put[b - 2], 16 * 2 * len(TERMS))
                        chain(v.tensor_copy(parts(0, b, 0), r))
                        chain(v.tensor_tensor(d1, r, parts(0, b, 0), ALU.subtract))
                        chain(v.tensor_copy(parts(0, b, 1), d1))
                        chain(v.tensor_tensor(r, d1, parts(0, b, 1), ALU.subtract))
                        v.tensor_copy(parts(0, b, 2), r).then_inc(qparts_ok, 1)
                        dve.wait_ge(qparts_ok, b + 1)
                    else:
                        if b == NB - 1:
                            dve.wait_ge(kparts_ok, NB)
                            v.memset(zeros, 0.0).then_inc(dve_const, 1)
                elif kind == "max":
                    _, u, m = s
                    j, i, k0, keys = max_pieces(u)[m]
                    w = wait_full(dve, s)
                    col = j * TB + i % TB
                    v.reduce_max(mpart[:, k0 // MW, u % 2, col:col + 1], w[:, 0:keys], AX.X).then_inc(free[ring[s] % 2], 1)
                elif kind == "maxend":
                    u = s[1]
                    last = max(ring[p] for p in (("max", u, m) for m in range(len(max_pieces(u)))))
                    for slot in range(2):
                        upto = last if last % 2 == slot else last - 1
                        dve.wait_ge(free[slot], upto // 2 + 1)
                    second = mpart[:, 1 if units()[u][0] * QB >= MW else 0, u % 2, :]
                    if u >= 2:
                        dve.wait_ge(nmp_ok, u - 1)
                    v.tensor_tensor(mx[:, u % 2, :], mpart[:, 0, u % 2, :], second, ALU.max).then_inc(mx_ok, 1)
                elif kind == "norm":
                    i = nth[s] % 2
                    w = wait_full(dve, s)
                    strips = w[:, :].rearrange("p (t h r) -> p t h r", t=2, h=H)
                    if nth[s] >= 2:
                        dve.wait_ge(full[ring[("ot",) + prev(s)] % 2], ring[("ot",) + prev(s)] // 2 + 1)
                    for t in range(2):
                        v.reciprocal(rl[:, t, :], strips[:, t, :, DK]).then_inc(dve_step, 1)
                        n[0] += 1
                    dve.wait_ge(dve_step, n[0])
                    for t in range(2):
                        ins = v.tensor_tensor(On[:, i, t * D:(t + 1) * D].rearrange("p (h d) -> p h d", h=H),
                                              strips[:, t, :, 0:DK],
                                              rl[:, t, :].rearrange("p (h o) -> p h o", o=1).to_broadcast([P, H, DK]),
                                              ALU.mult).then_inc(on_ok, 1)
                    dve.wait_ge(on_ok, 2 * (nth[s] + 1))
                    release(dve, s)
                elif kind == "wo":
                    _, b, h2 = s
                    t0 = TB * b + 2 * h2
                    w = wait_full(dve, s)
                    v.tensor_tensor(X[:, t0:t0 + 2, :], w[:, 0:2 * D].rearrange("p (t d) -> p t d", t=2),
                                    X[:, t0:t0 + 2, :], ALU.add).then_inc(x2_ok, 1)
                    dve.wait_ge(x2_ok, nth[s] + 1)
                    release(dve, s)
                    for t in range(t0, t0 + 2):
                        chain(v.bn_stats(stats[:, t, :], X[:, t, :]))
                    for t in range(t0, t0 + 2):
                        chain(v.bn_aggr(mv[:, 1, t, :], stats[:, t, :]))
                    if h2 == 1:
                        dve.sem_inc(stats2_ok, 1)
                elif kind == "h2t":
                    b = s[1]
                    dve.wait_ge(rstd_ok, NB + b + 1)
                    for t in range(TB * b, TB * (b + 1)):
                        chain(v.tensor_scalar(XN[:, t, :], X[:, t, :], mv[:, 1, t, 0:1], rstd[:, 1, t:t + 1],
                                              ALU.subtract, ALU.mult))
                    dve.sem_inc(xn2_ok, 1)
                elif kind == "logit":
                    b = s[1]
                    w = wait_full(dve, s)
                    chain(v.tensor_copy(LG[:, TB * b:TB * (b + 1), :],
                                        w[:, 0:TB * E].rearrange("p (t e) -> p t e", t=TB)))
                    release(dve, s)
                    for t in range(TB * b, TB * (b + 1)):
                        v.max(T8[:, t, :], LG[:, t, :]).then_inc(dve_step, 1)
                    n[0] += TB
                    dve.wait_ge(dve_step, n[0])
                    for t in range(TB * b, TB * (b + 1)):
                        v.max_index(I8[:, t, :], T8[:, t, :], LG[:, t, :]).then_inc(dve_step, 1)
                    n[0] += TB
                    dve.wait_ge(dve_step, n[0])
                elif kind == "rank":
                    v.tensor_tensor(wt[:, 0, :], T8[:, :, 1], T8[:, :, 0], ALU.subtract).then_inc(diff_ok, 1)
                    for k in range(TOPK):
                        chain(v.tensor_copy(idxf[:, k, :], I8[:, :, k]))
                    flat_idx = idxf[:, :, :].rearrange("p k t -> p (k t)")
                    for e in range(E):
                        v.tensor_scalar(OH[:, e].rearrange("p k t -> p (k t)"), flat_idx, io[:, e:e + 1], None,
                                        ALU.is_equal).then_inc(oh_ok, 1)
                    w = wait_full(dve, s)
                    dve.wait_ge(restart_ok, 1)
                    n_oh = E * TOPK * NT
                    local, total = w[:, 0:n_oh], w[:, QB:QB + n_oh]
                    fl = incl.rearrange("p e n -> p (e n)")
                    chain(v.tensor_tensor_scan(fl, restart.rearrange("p e n -> p (e n)"), total, 0.0,
                                               ALU.mult, ALU.add))
                    chain(v.tensor_tensor(fl, fl, total, ALU.subtract))
                    chain(v.tensor_tensor(fl, fl, local, ALU.add))
                    chain(v.tensor_tensor(fl, fl, OH.rearrange("p e k t -> p (e k t)"), ALU.mult))
                    release(dve, s)
                    chain(v.tensor_reduce(rk[:, :], incl.rearrange("p e n -> p n e"), AX.X, ALU.add))
                    chain(v.tensor_scalar(keep[:, :], rk[:, :], float(CAP), None, ALU.is_lt))
                    chain(v.scalar_tensor_tensor(slotf[:, 0, :], flat_idx, float(CAP), rk[:, :], ALU.mult, ALU.add))
                    chain(v.tensor_scalar(slotf[:, 1, :], slotf[:, 0, :], float(2 * NSLOT), None, ALU.add))
                    chain(v.scalar_tensor_tensor(slotf[:, 2, :], keep[:, :], float(-2 * NSLOT), slotf[:, 1, :],
                                                 ALU.mult, ALU.add))
                    chain(v.tensor_copy(put_at[:, :], slotf[:, 2, :]))
                    chain(v.tensor_tensor(slotf[:, 1, :], slotf[:, 0, :], keep[:, :], ALU.mult))
                    v.tensor_copy(get_at[:, :], slotf[:, 1, :]).then_inc(idx_ok, 1)
                    dve.wait_ge(ediff_ok, 1)
                    chain(v.tensor_scalar(wt[:, 2, :], wt[:, 1, :], 1.0, None, ALU.add))
                    chain(v.reciprocal(wt[:, 3, :], wt[:, 2, :]))
                    chain(v.tensor_tensor(wt[:, 4, :], wt[:, 3, :], wt[:, 1, :], ALU.mult))
                    for k in range(TOPK):
                        v.tensor_tensor(wk_[:, k, :], wt[:, 3 + k, :], keep[:, k * NT:(k + 1) * NT],
                                        ALU.mult).then_inc(wts_ok, 1)

            dve.wait_ge(scattered, 16)
            for e in range(E + 1):
                if e < E:
                    dve.wait_ge(xbt_ps, e + 1)
                    if e >= 2:
                        for i in range(2):
                            dve.wait_ge(up_full[i], (e - 1) * NF // 2)
                    v.tensor_copy(XBT[:, e % 2, 0:QB], SC[0][:, :]).then_inc(xbt_ok, 1)
                    v.tensor_copy(XBT[:, e % 2, QB:CAP], SC[1][:, 0:CAP - QB]).then_inc(xbt_ok, 1)
                if e >= 1:
                    f = e - 1
                    dve.wait_ge(down_ps, f + 1)
                    if f >= 2:
                        dve.wait_ge(yb_out[f % 2], 16 * (f // 2))
                    v.tensor_copy(YB[:, f % 2, 0:4, :], AV[:, :].rearrange("p (t d) -> p t d", t=4)).then_inc(dve_step, 1)
                    v.tensor_copy(YB[:, f % 2, 4, :], SC[2][:, 0:D]).then_inc(dve_step, 1)
                    n[0] += 2
                    dve.wait_ge(dve_step, n[0])
                    dve.sem_inc(yb_ok, 1)
            dve.wait_ge(wts_ok, TOPK)
            for t in range(NT):
                dve.wait_ge(gathered[t], 16 * TOPK)
                chain(v.scalar_tensor_tensor(X[:, t, :], GY[:, TOPK * t, :], wk_[:, 0, t:t + 1], X[:, t, :],
                                             ALU.mult, ALU.add))
                v.scalar_tensor_tensor(X[:, t, :], GY[:, TOPK * t + 1, :], wk_[:, 1, t:t + 1], X[:, t, :],
                                       ALU.mult, ALU.add).then_inc(out_ok, 1)

        @block.tensor
        def _(pe):
            t_ = nc.tensor

            def take(step):
                r = ring[step]
                if r >= 2:
                    pe.wait_ge(free[r % 2], r // 2)
                return WK[r % 2], full[r % 2]

            pe.wait_ge(const_ok, 1)
            for s in plan:
                kind = s[0]
                if kind == "mod":
                    w, ok = take(s)
                    pe.wait_ge(silu_ok, 1)
                    t_.matmul(w[:, 0:QB], silu_b[:, :], wm[:, 0:QB], start=True, stop=True)
                    t_.matmul(w[:, QB:6 * D], silu_b[:, :], wm[:, QB:6 * D], start=True, stop=True)
                    for i in range(2):
                        last = t_.matmul(w[:, 6 * D + i:6 * D + i + 1], wm[:, i * D:(i + 1) * D], silu_b[:, 0:1],
                                         start=True, stop=True)
                    last.then_inc(ok, 1)
                elif kind == "xt":
                    b = s[1]
                    w, ok = take(s)
                    pe.wait_ge(xn_ok, TB * (b + 1))
                    for t in range(TB):
                        last = t_.transpose(w[:, t * P:(t + 1) * P], XN[:, TB * b + t, :], ident[:, :])
                    last.then_inc(ok, 1)
                elif kind in ("q", "k"):
                    b, i = s[1], int(kind == "k")
                    w, ok = take(s)
                    r = ring[("xt", b)]
                    pe.wait_ge(free[r % 2], r // 2 + 1)
                    pe.wait_ge(rot_ok, 4)
                    t_.matmul(w[:, 0:QB], wsb[:, i, :], hT[:, QB * b:QB * (b + 1)], start=True, stop=True)
                    t_.matmul(w[:, QB:2 * QB], wsb[:, 4 + i, :], hT[:, QB * b:QB * (b + 1)], start=True,
                              stop=True).then_inc(ok, 1)
                elif kind == "v":
                    b = s[1]
                    w, ok = take(s)
                    for t in range(TB):
                        last = t_.matmul(w[:, t * P:(t + 1) * P], hT[:, (TB * b + t) * P:(TB * b + t + 1) * P],
                                         wsb[:, 2, :], start=True, stop=True)
                    last.then_inc(ok, 1)
                elif kind in ("max", "max2"):
                    _, u, m = s
                    b, g = units()[u]
                    j, i, k0, keys = max_pieces(u)[m]
                    h = GH * g + j
                    if kind == "max":
                        w, ok = take(s)
                        c0 = 0
                    else:
                        c0 = QB
                    if u == 0 and m == 0:
                        pe.wait_ge(ones_in, 32)
                    if m == 0 and g == 0 and c0 == 0:
                        pe.wait_ge(qk_got[b], 16 * (4 if b < 2 else 6))
                    nk = min(QB, keys - c0)
                    ends = k0 + c0 + nk == P * (i + 1)
                    last = t_.matmul(w[:, c0:c0 + nk], QP[:, h % 2, h // 2, b % 2, (i % TB) * P:(i % TB + 1) * P],
                                     KS[:, h // 2, k0 + c0:k0 + c0 + nk], start=True, stop=not ends)
                    if ends:
                        last = t_.matmul(w[:, c0 + nk - P:c0 + nk], identb[:, :], causal[:, :],
                                         start=False, stop=True)
                    if c0 + nk == keys:
                        last.then_inc(ok, 1)
                elif kind == "negmax":
                    u = s[1]
                    w, ok = take(s)
                    pe.wait_ge(nmp_ok, u + 1)
                    t_.transpose(w[0:3 * GH * TB, 0:P // 2].bitcast(bf16),
                                 nmp[:, u % 2, :, :].rearrange("p r n -> p (r n)"), identb[:, :]).then_inc(ok, 1)
                elif kind == "score":
                    _, u, kt, j = s
                    b, g = units()[u]
                    q0 = first_column(u, kt)
                    if kt == 0 and j == 0:
                        pe.wait_ge(m_got[u % 2], 32 * (u // 2 + 1))
                    h = GH * g + j
                    t = st.tile[u, kt, j]
                    if t >= 3:
                        pe.wait_ge(exped, t - 2)
                    t_.matmul(SC[t % 3][:, q0:QB], KS[:, h // 2, kt * P:(kt + 1) * P],
                              QP[:, h % 2, h // 2, b % 2, q0:QB], start=True, stop=True).then_inc(scored, 1)
                elif kind == "av":
                    _, u, kt = s
                    b, g = units()[u]
                    q0 = first_column(u, kt)
                    pe.wait_ge(exped, st.tile[u, kt, GH - 1] + 1)
                    if (u, kt, GH - 1) in st.diag:
                        pe.wait_ge(masked, st.diag[u, kt, GH - 1])
                    if u == 0 and kt == 0:
                        pe.wait_ge(dve_const, 1)
                    if g == 0 and kt == TB * b:
                        r = ring[("v", b)]
                        pe.wait_ge(free[r % 2], r // 2 + 1)
                    if kt == 0 and u >= 1:
                        pe.wait_ge(evaced, u)
                    for j in range(GH):
                        last = t_.matmul(AV[32 * j:32 * j + DK + 1, q0:QB], VX[:, kt, GH * g + j, :],
                                         PRB[:, st.tile[u, kt, j] % PR, q0:QB], start=(kt == 0),
                                         stop=(kt == TB * (b + 1) - 1))
                    last.then_inc(av_ok, 1)
                elif kind == "norm":
                    _, b, h2 = s
                    w, ok = take(s)
                    pe.wait_ge(evaced, NG * (b + 1))
                    for t in range(2):
                        for g in range(NG):
                            c0 = (2 * h2 + t) * P
                            last = t_.transpose(w[:, t * QB + g * P:t * QB + (g + 1) * P], OT[:, g, c0:c0 + P],
                                                ident[:, :])
                    last.then_inc(ok, 1)
                    pe.wait_ge(ok, ring[s] // 2 + 1)
                    pe.sem_inc(norm_read, 1)
                elif kind == "ot":
                    w, ok = take(s)
                    pe.wait_ge(on_ok, 2 * (nth[s] + 1))
                    for t in range(2):
                        last = t_.transpose(w[:, t * P:(t + 1) * P], On[:, nth[s] % 2, t * D:(t + 1) * D], ident[:, :])
                    last.then_inc(ok, 1)
                elif kind == "wo":
                    w, ok = take(s)
                    r = ring[("ot",) + s[1:]]
                    pe.wait_ge(free[r % 2], r // 2 + 1)
                    pe.wait_ge(wo_ok, 1)
                    for t in range(2):
                        last = t_.matmul(w[:, t * P:(t + 1) * P], OnT[:, nth[s] % 2, t * P:(t + 1) * P],
                                         wsb[:, 3, :], start=True, stop=True)
                    last.then_inc(ok, 1)
                elif kind == "h2t":
                    b = s[1]
                    w, ok = take(s)
                    pe.wait_ge(h2_ok, b + 1)
                    for t in range(TB):
                        last = t_.transpose(w[:, t * P:(t + 1) * P], XN[:, TB * b + t, :], ident[:, :])
                    last.then_inc(ok, 1)
                elif kind == "logit":
                    b = s[1]
                    w, ok = take(s)
                    r = ring[("h2t", b)]
                    pe.wait_ge(free[r % 2], r // 2 + 1)
                    pe.wait_ge(wg_in, 16)
                    for t in range(TB):
                        last = t_.matmul(w[:, t * E:(t + 1) * E], hT[:, (TB * b + t) * P:(TB * b + t + 1) * P],
                                         wg[:, :], start=True, stop=True)
                    last.then_inc(ok, 1)
                elif kind == "rank":
                    w, ok = take(s)
                    pe.wait_ge(oh_ok, E)
                    oh = OH.rearrange("p e k t -> p (e k t)")
                    t_.matmul(w[:, 0:E * TOPK * NT], before[:, :], oh, start=True, stop=True)
                    t_.matmul(w[:, QB:QB + E * TOPK * NT], ones[:, :], oh, start=True, stop=True).then_inc(ok, 1)

            def turn(e):
                pe.wait_ge(xb_in[e % 2], 16 * (e // 2 + 1))
                if e == 0:
                    pe.wait_ge(exped, len(st.tile))
                else:
                    pe.wait_ge(xbt_ok, 2 * e)
                for t in range(CT):
                    dst = SC[0][:, t * P:(t + 1) * P] if t < 4 else SC[1][:, 0:P]
                    last = t_.transpose(dst, XB[:, e % 2, t, :], ident[:, :])
                last.then_inc(xbt_ps, 1)

            for i in range(2):
                last_use = (NRING - 1) if (NRING - 1) % 2 == i else NRING - 2
                pe.wait_ge(free[i], last_use // 2 + 1)
            pe.wait_ge(w1_in, 16)
            pe.wait_ge(w2_ok, E)
            pe.wait_ge(evaced, NU)
            turn(0)
            for e in range(E):
                pe.wait_ge(xbt_ok, 2 * (e + 1))
                for f in range(NF):
                    m = e * NF + f
                    if m >= 2:
                        pe.wait_ge(up_free[m % 2], m // 2)
                    for i in range(2):
                        last = t_.matmul(WK[m % 2][:, i * QB:i * QB + CAP // 2], W1[:, e, f * P:(f + 1) * P],
                                         XBT[:, e % 2, i * CAP // 2:(i + 1) * CAP // 2], start=True, stop=True)
                    last.then_inc(up_full[m % 2], 1)
                if e + 1 < E:
                    turn(e + 1)
                for i in range(2):
                    pe.wait_ge(up_free[i], (e + 1) * NF // 2)
                if e >= 1:
                    pe.wait_ge(yb_ok, e)
                for t in range(CT):
                    dst = AV[:, t * D:(t + 1) * D] if t < 4 else SC[2][:, 0:D]
                    for f in range(NF):
                        last = t_.matmul(dst, HG[:, e % 2, f, t * P:(t + 1) * P], W2[:, e, f, :],
                                         start=(f == 0), stop=(f == NF - 1))
                last.then_inc(down_ps, 1)


_INS = ["L0_attn_x", "L0_attn_Wq", "L0_attn_Wk", "L0_attn_Wv", "L0_attn_Wo", "L0_ffn_w_g", "L0_ffn_c_fc",
        "L0_ffn_c_proj", "L0_c", "L0_wmod"]


def rotary_tables():
    inv = (1.0 / np.float32(10000.0) ** (np.arange(0, DK, 2, dtype=np.float32) / np.float32(DK))).astype(np.float32)
    ang = np.outer(np.arange(S, dtype=np.float32), inv).astype(np.float32)
    cos, sin = (np.repeat(f(ang).astype(np.float32), 2, axis=-1).T for f in (np.cos, np.sin))
    return np.ascontiguousarray(np.tile(cos, (H, 1))), np.ascontiguousarray(np.tile(sin, (H, 1)))


def kernel(**inputs):
    import concourse.bacc as _bacc
    from concourse import mybir as _mybir
    from concourse.bass_utils import run_bass_kernel_spmd as _run

    nc = _bacc.Bacc("TRN2", target_bir_lowering=False, num_devices=1)
    arrays, args = {}, []
    for name in _INS:
        arrays[f"in_{name}_dram"] = np.ascontiguousarray(inputs[name])
    arrays["rope_cos"], arrays["rope_sin"] = rotary_tables()
    import ml_dtypes
    pad = np.zeros((64 - ROWS, NPAIR * S), ml_dtypes.bfloat16)
    pad[0:3] = 1.0
    arrays["pad_rows"] = pad
    for name, a in arrays.items():
        args.append(nc.dram_tensor(name, a.shape, _mybir.dt.from_np(a.dtype), kind="ExternalInput").ap())
    args.append(nc.dram_tensor("out_dram", (1, S, D), _mybir.dt.float32, kind="ExternalOutput").ap())
    block_kernel(nc, *args)
    r = _run(nc, [arrays], core_ids=[0])
    return r.results[0]["out_dram"]
```

```python
import numpy as np
import concourse.bass as bass
from concourse import mybir
from contextlib import ExitStack

P = 128
S = 2048
D = 128
H = 16
DK = D // H
NT = S // P
QB = 512
NB = S // QB
TB = QB // P
GH = 4
NG = H // GH
NU = NB * NG
NPAIR = H // 2
E = 8
TOPK = 2
F = 4 * D
NF = F // P
CAP = 2 * int(1.25 * S) // E
CT = CAP // P
NSLOT = E * CAP
ROW = D + 2
NOWHERE = 1e6
SCALE = float(DK) ** -0.5
EPS = 1e-5

TERMS = [(0, 0), (0, 1), (1, 0), (1, 1), (0, 2), (2, 0)]
ROWS = DK * len(TERMS)
KROWS = ROWS + 3
NW = 4
PR = 16
RINGLESS = ("ln", "xn", "score", "av", "evac", "maxend", "h2", "scatter")
EPI = {"norm": 10, "ot": 52, "wo": 66, "h2": 77, "h2t": 102, "logit": 127, "rank": 155, "scatter": 185}
PIECE = 80
LEAD = 10000
AVLAG = 2


def units():
    return [(b, g) for b in range(NB) for g in range(NG)]


def max_pieces(u):
    b, _ = units()[u]
    pieces = []
    for i in range(TB * b, TB * (b + 1)):
        pieces += [((j,), i, k0, QB) for k0 in range(0, QB * b, QB) for j in range(GH)]
        keys = P * (i + 1) - QB * b
        n = QB // keys
        pieces += [(tuple(range(j, min(j + n, GH))), i, QB * b, keys) for j in range(0, GH, n)]
    return pieces


BATCHES = [(TB * b, TB) for b in range(NB - 1)] + [(TB * (NB - 1), TB // 2), (TB * (NB - 1) + TB // 2, TB // 2)]
HALF = BATCHES[-1][0] - 1


def epilogue(b):
    n = BATCHES[b][1]
    return ([("norm", b, t) for t in range(n)] + [("ot", b), ("wo", b), ("h2", b), ("h2t", b), ("logit", b), ("rank", b)]
            + [("scatter", b, m) for m in range(TOPK * n)])


def last_epilogues():
    one, two = epilogue(NB - 1), epilogue(NB)
    order = [("ot", one), ("norm", two), ("wo", one), ("ot", two), ("h2", one), ("wo", two), ("h2t", one), ("h2", two),
             ("logit", one), ("rank", one), ("h2t", two), ("logit", two), ("scatter", one), ("rank", two),
             ("scatter", two)]
    return [step for kind, steps in order for step in steps if step[0] == kind]


def projections(b):
    return [("q", b), ("qr", b), ("k", b), ("kr", b), ("v", b)]


BETWEEN = [(8, 4, projections(1)[:4] + [("xt", 2), ("v", 1), ("xt", 3)]), (1, 1, [("xn", 1), ("xt", 1)]), (4, 2, [("v", 0), ("xn", 2), ("xn", 3)]), (56, 6, projections(2)),
           (92, 6, projections(3))]


EXPAND = {3: 2, 4: 3}


def make_plan():
    plan = [("ln", 0), ("xt", 0), ("mod", 0)] + projections(0)[:4] + [("ln", 1), ("mod", 1)]
    pieces = [(u, n) for u in range(NU) for n in range(len(max_pieces(u)))]
    at = 0
    done = 0.0
    later = []

    def cost(u, n):
        heads, _, _, keys = max_pieces(u)[n]
        return len(heads) * keys + PIECE

    def put_off(ticks, step):
        later.append([ticks, step])
        later.sort(key=lambda x: x[0])

    def tick():
        for x in later:
            x[0] -= 1
        if later and later[0][0] <= 0:
            plan.append(later.pop(0)[1])

    def piece():
        nonlocal at, done
        u, n = pieces[at]
        plan.append(("max", u, n))
        done += cost(u, n)
        at += 1
        if at == len(pieces) or pieces[at][0] > u:
            plan.append(("maxend", u))
            put_off(14 if u else 12, ("negmax", u))
        tick()

    cum_m, cum_s = [0], [0]
    for u, (b, _) in enumerate(units()):
        cum_m.append(cum_m[-1] + sum(cost(*p) for p in pieces if p[0] == u))
        cum_s.append(cum_s[-1] + GH * sum(QB - first_column(u, kt) for kt in range(TB * (b + 1))))
    for first, apart, steps in BETWEEN:
        for n, step in enumerate(steps):
            put_off(first + apart * n, step)
    while pieces[at][0] == 0:
        piece()
    avs = []
    for u, (b, g) in enumerate(units()):
        while at < len(pieces) and pieces[at][0] <= u:
            piece()
        while ("negmax", u) not in plan:
            if at < len(pieces) and pieces[at][0] <= u + 1:
                piece()
            else:
                plan.append(later.pop(0)[1])
        rate, base, went = 0.0, done, 0
        for v in range(u + 1, NU):
            due = max(cum_s[v] - LEAD, cum_s[u] + (cum_s[u + 1] - cum_s[u]) * 0.5)
            rate = max(rate, (cum_m[v + 1] - done) / (due - cum_s[u]))
        for kt in range(TB * (b + 1)):
            for j in range(GH):
                plan.append(("score", u, kt, j))
                went += QB - first_column(u, kt)
                tick()
                while at < len(pieces) and done < base + rate * went:
                    piece()
            avs.append((u, kt))
            while len(avs) > AVLAG + (avs[0][1] == 0) and avs[0] != (NU - 1, HALF):
                uu, kk = avs.pop(0)
                plan.append(("av", uu, kk))
                if kk == TB * (units()[uu][0] + 1) - 1:
                    plan.append(("evac", uu))
                    if uu % NG == NG - 1:
                        for step in epilogue(uu // NG):
                            put_off(EPI[step[0]] + 6 * (step[-1] if len(step) == 3 else 0), step)
    assert avs[0] == (NU - 1, HALF)
    plan += [("av", NU - 1, HALF)] + [x[1] for x in later] + [("evac", NU - 1)]
    plan += epilogue(NB - 1)[:TB // 2] + [("tail", 0)] + last_epilogues()
    assert plan.index(("v", NB - 1)) < plan.index(("norm", 0, 0))
    return plan


def first_column(u, kt):
    return P * max(0, kt - TB * units()[u][0])


class Steps:

    def __init__(self):
        self.plan = make_plan()
        self.ring = {s: n for n, s in enumerate(x for x in self.plan if x[0] not in RINGLESS)}
        self.tile = {}
        for s in self.plan:
            if s[0] == "score":
                self.tile[s[1:]] = len(self.tile)
        self.diag = {}
        for s in self.plan:
            if s[0] == "score" and s[2] >= TB * units()[s[1]][0]:
                self.diag[s[1:]] = len(self.diag) + 1


def block_kernel(nc, x, Wq, Wk, Wv, Wo, w_g, c_fc, c_proj, c, wmod, cos_t, sin_t, pad_t, out):
    f32, bf16, u32 = mybir.dt.float32, mybir.dt.bfloat16, mybir.dt.uint32
    ALU, ACT, AX = mybir.AluOpType, mybir.ActivationFunctionType, mybir.AxisListType
    st = Steps()
    plan, ring = st.plan, st.ring
    NRING = len(ring)

    q_rows = nc.dram_tensor("q_rows", (H, ROWS, S), bf16)
    k_rows = nc.dram_tensor("k_rows", (H, ROWS, S), bf16)
    m_rows = nc.dram_tensor("m_rows", (NU, 3 * TB * GH, P), bf16)
    slots_x = nc.dram_tensor("slots_x", (NSLOT, ROW), f32)
    parts_y = nc.dram_tensor("parts_y", (TOPK * S, D), f32)

    ctx = ExitStack()
    with ctx:
        def sb(name, shape, dt=f32):
            return ctx.enter_context(nc.sbuf_tensor(name, shape, dt))

        def sem(name):
            return ctx.enter_context(nc.semaphore(name))

        X = sb("X", [P, NT, D])
        XN = sb("XN", [P, NT, ROW])
        hT = sb("hT", [P, S])
        KS = sb("KS", [P, NPAIR, S], bf16)
        QP = sb("QP", [P, 2, NPAIR, 2, QB], bf16)
        VX = sb("VX", [P, NT, H, DK + 1])
        PRB = sb("PRB", [P, PR, QB])
        part_set = sb("part_set", [P, 2, 2, 3, QB], bf16)
        CS = sb("CS", [P, 2, S])
        W1 = CS[:, :, :].rearrange("p a s -> p (a s)").rearrange("p (e f) -> p e f", e=E)
        W2 = sb("W2", [P, E, NF, D])
        OT = sb("OT", [P, NG, QB])
        RT = sb("RT", [P, 2, 3, QB])
        wsb = sb("wsb", [P, 6, D])
        wg = sb("wg", [P, E])
        wm = PRB[:, 0:2, :].rearrange("p a b -> p (a b)")[:, 0:6 * D]
        MODB = sb("MODB", [P, 2, D])
        modT = sb("modT", [P, 4])
        ccol = sb("ccol", [P, 4])
        silu_b = sb("silu_b", [P, P])
        sign = sb("sign", [P, D])
        stats = sb("stats", [P, NT, 6])
        mv = sb("mv", [P, 2, NT, 2])
        veps = sb("veps", [P, NT])
        half = sb("half", [P, NT])
        rstd = sb("rstd", [P, 2, NT])
        ident = sb("ident", [P, P])
        identb = sb("identb", [P, P], bf16)
        causal = sb("causal", [P, P], bf16)
        before = sb("before", [P, P])
        ones = sb("ones", [P, P])
        mpart = sb("mpart", [P, 2, GH * TB, NB])
        mx = sb("mx", [P, 2, GH * TB])
        nm = sb("nm", [P, 2, 3, GH * TB])
        nmp = sb("nmp", [P, 2, 3, GH * TB], bf16)
        mrow = sb("mrow", [3 * GH * TB, 2, P], bf16)
        rl = sb("rl", [P, 2, H])
        LG = sb("LG", [P, TB, E])
        T8 = sb("T8", [P, TB, 8])
        I8 = sb("I8", [P, TB, 8], u32)
        io = sb("io", [P, E])
        idx_s, rk_s, keep_s = (sb(n, [P, TOPK * TB]) for n in ("idx_s", "rk_s", "keep_s"))
        OH_s, incl_s, before_s, restart = (sb(n, [P, E * TOPK * TB]) for n in ("OH_s", "incl_s", "before_s", "restart"))
        count = sb("count", [P, E, TOPK])
        restart_half = sb("restart_half", [P, E * TOPK * TB // 2])
        first_s = sb("first_s", [P, E * TB])
        taken = sb("taken", [P, TB])
        slot_s = sb("slot_s", [P, 3, TOPK * TB])
        put_at = sb("put_at", [P, 2, TOPK * TB], u32)
        back_to = sb("back_to", [P, E, CT], u32)
        row_id = sb("row_id", [P, TOPK, NT])
        row_u = sb("row_u", [P, TOPK, NT], u32)
        wt = sb("wt", [P, 3, TB])
        rt_flat = RT[:, :, :, :].rearrange("p a b n -> p (a b n)")
        empty = rt_flat[:, 0:CT * ROW].rearrange("p (t d) -> p t d", t=CT)
        XK = rt_flat[:, 4 * QB:4 * QB + TB * ROW].rearrange("p (t d) -> p t d", t=TB)
        On = rt_flat[:, 2 * QB:3 * QB].rearrange("p (t d) -> p t d", t=TB)
        OnT = rt_flat[:, 3 * QB:4 * QB]
        flat = KS[:, :, :].rearrange("p a s -> p (a s)").bitcast(f32)
        XB = flat[:, 0:2 * CT * ROW].rearrange("p (n t d) -> p n t d", n=2, t=CT)
        XBT = flat[:, 3 * CAP:5 * CAP].rearrange("p (n s) -> p n s", n=2)
        YB = flat[:, 5 * CAP:7 * CAP].rearrange("p (n t d) -> p n t d", n=2, t=CT)
        flatq = QP[:, :, :, :, :].rearrange("p c h a s -> p (c h a s)").bitcast(f32)
        HG = flatq[:, 0:2 * NF * CAP].rearrange("p (n f s) -> p n f s", n=2, f=NF)
        GY = PRB[:, :, :].rearrange("p a b -> p (a b)")[:, 0:TOPK * NT * D].rearrange("p (k t d) -> p k t d", k=TOPK, t=NT)

        WK = ctx.enter_context(nc.psum_tensor("work", [P, NW, QB], f32))
        SC = [ctx.enter_context(nc.psum_tensor(f"score{i}", [P, QB], f32)) for i in range(3)]
        AV = ctx.enter_context(nc.psum_tensor("av", [P, QB], f32))

        qp_zero = sem("qp_zero")
        w_in, mod_in, ones_in, w2_in, w1_in = (
            sem(n) for n in ("w_in", "mod_in", "ones_in", "w2_in", "w1_in"))
        x_in = [sem(f"x_in{b}") for b in range(NB)]
        rope_in = [sem(f"rope_in{b}") for b in range(NB)]
        wm_in, wqk_in = sem("wm_in"), sem("wqk_in")
        first_part, first_rest = sem("first_part"), sem("first_rest")
        wg_in, zero_out, parts_zero = sem("wg_in"), sem("zero_out"), sem("parts_zero")
        k_first_put = sem("k_first_put")
        qk_put = [sem(f"qk_put{b}") for b in range(NB)]
        qk_got = [sem(f"qk_got{b}") for b in range(NB)]
        qk_more = [sem(f"qk_more{b}") for b in range(NB)]
        m_put, m_got = [sem(f"m_put{i}") for i in range(2)], [sem(f"m_got{i}") for i in range(2)]
        const_ok = sem("const_ok")
        pool_step = sem("pool_step")
        dve_step = sem("dve_step")
        dve_const = sem("dve_const")
        act_silu = sem("act_silu")
        silu_ok = sem("silu_ok")
        rot_ok = sem("rot_ok")
        stats_ok, rstd_ok, xn_ok = sem("stats_ok"), sem("rstd_ok"), sem("xn_ok")
        modt_ok, modb_ok = sem("modt_ok"), sem("modb_ok")
        full = [sem(f"full{i}") for i in range(NW)]
        free = [sem(f"free{i}") for i in range(NW)]
        roped, kparts_ok, qparts_ok = (
            sem(n) for n in ("roped", "kparts_ok", "qparts_ok"))
        mx_ok, nmp_ok, mrow_ok = sem("mx_ok"), sem("nmp_ok"), sem("mrow_ok")
        scored, exped, masked, av_ok, evaced = (
            sem(n) for n in ("scored", "exped", "masked", "av_ok", "evaced"))
        stats2_ok, h2_ok = sem("stats2_ok"), sem("h2_ok")
        wo_ok, w2_ok = sem("wo_ok"), sem("w2_ok")
        diff_ok, ediff_ok, oh_ok, rows_ok = (sem(n) for n in ("diff_ok", "ediff_ok", "oh_ok", "rows_ok"))
        scattered, xk_ok = sem("scattered"), sem("xk_ok")
        xb_in = [sem(f"xb_in{i}") for i in range(2)]
        xbt_ps, xbt_ok = sem("xbt_ps"), sem("xbt_ok")
        up_full, up_free = [sem(f"up_full{i}") for i in range(2)], [sem(f"up_free{i}") for i in range(2)]
        down_ps, yb_ok = sem("down_ps"), sem("yb_ok")
        last_ps, last_ok = sem("last_ps"), sem("last_ok")
        yb_out = [sem(f"yb_out{i}") for i in range(2)]
        parts_in = [sem(f"parts_in{b}") for b in range(NB)]
        out_ok, out_done = sem("out_ok"), sem("out_done")

        block = ctx.enter_context(nc.Block())

        def wait_full(eng, step):
            eng.wait_ge(full[ring[step] % NW], ring[step] // NW + 1)
            return WK[:, ring[step] % NW, :]

        def wait_read(eng, step):
            eng.wait_ge(free[ring[step] % NW], ring[step] // NW + 1)

        def on_tile(b, t):
            return (BATCHES[b][0] + t) % TB

        N_FIRST = sum(part == 0 for _, part in TERMS)

        def puts(b):
            return 2 * len(TERMS) - (N_FIRST if b == 0 else 0)

        def last_bank(t):
            return (AV[:, 0:D], SC[2][:, 0:D], WK[:, 0, 0:D], WK[:, 1, 0:D], WK[:, 2, 0:D])[t]

        def parts(which, b, r):
            return part_set[:, which, b % 2, r, :]

        def release(eng, s):
            eng.sem_inc(free[ring[s] % NW], 1)

        q_pairs = q_rows.ap().rearrange("(a b) r s -> b r a s", b=2)
        k_pairs = k_rows.ap().rearrange("(a b) r s -> b r a s", b=2)

        @block.sync
        def _(sp):
            x_t = x[0].rearrange("(t p) d -> p t d", p=P)
            def load_block(b):
                sp.dma_start(X[:, TB * b:TB * (b + 1), :], x_t[:, TB * b:TB * (b + 1), :]).then_inc(x_in[b], 16)
                for n, table in enumerate((cos_t, sin_t)):
                    cols = slice(QB * b, QB * (b + 1))
                    sp.dma_start(CS[:, n, cols], table[:, cols]).then_inc(rope_in[b], 16)
                    if b == 0 and n == 0:
                        sp.dma_start(ccol[:, 0:1], c.rearrange("a p -> p a")).then_inc(mod_in, 16)
                        sp.dma_start(wm[:, :], wmod).then_inc(wm_in, 16)
                        for i, w in enumerate((Wq, Wk)):
                            sp.dma_start(wsb[:, i, :], w).then_inc(wqk_in, 16)

            load_block(0)
            load_block(1)
            for i, w in enumerate((Wv, Wo)):
                sp.dma_start(wsb[:, 2 + i, :], w).then_inc(w_in, 16)
            for par in range(2):
                sp.dma_start(KS[64 * par + ROWS:64 * (par + 1), :, :],
                             pad_t.rearrange("r (a s) -> r a s", a=NPAIR)).then_inc(ones_in, 16)
            sp.dma_start(wg[:, :], w_g).then_inc(wg_in, 16)
            load_block(2)
            load_block(3)

            def expand(b):
                cols = slice(QB * b, QB * (b + 1))
                for n, (a, i) in enumerate((a, i) for a in range(3) for i in range(2)):
                    if b == 0:
                        if (a, i) == (0, 1):
                            continue
                        sp.wait_ge(first_part, n + 1)
                    elif a == 0 and i == 0:
                        sp.wait_ge(qparts_ok, b)
                        sp.wait_ge(kparts_ok, b)
                    for t, term in enumerate(TERMS):
                        if term[i] == a:
                            sp.dma_start((q_rows, k_rows)[i][:, DK * t:DK * (t + 1), cols],
                                         parts(i, b, a)).then_inc(qk_put[b], 16)
                if b == 0:
                    sp.wait_ge(k_first_put, 16 * N_FIRST)
                sp.wait_ge(qk_put[b], 16 * puts(b))
                if b < 2:
                    sp.wait_ge(qp_zero, 4)
                for n, pairs in enumerate((slice(0, NPAIR // 2), slice(NPAIR // 2, NPAIR))):
                    for par in range(2):
                        sp.dma_start(KS[64 * par:64 * par + ROWS, pairs, cols],
                                     k_pairs[par, :, pairs, cols]).then_inc((qk_got, qk_more)[n][b], 16)
                        if b < 2:
                            sp.dma_start(QP[64 * par:64 * par + ROWS, par, pairs, b, :],
                                         q_pairs[par, :, pairs, cols]).then_inc((qk_got, qk_more)[n][b], 16)

            def put_negmax(u):
                b, g = units()[u]
                sp.wait_ge(mrow_ok, u + 1)
                sp.dma_start(m_rows[u], mrow[:, u % 2, :]).then_inc(m_put[u % 2], 16)
                sp.wait_ge(m_put[u % 2], 16 * (u // 2 + 1))
                src = m_rows[u].rearrange("(r a b i) q -> b r a (i q)", r=3, a=2, b=2)
                for par in range(2):
                    sp.dma_start(QP[64 * par + ROWS:64 * par + KROWS, par, 2 * g:2 * g + 2, b % 2, :],
                                 src[par]).then_inc(m_got[u % 2], 16)

            for b in range(2):
                expand(b)
                put_negmax(b)
            def load_w2(n):
                two = slice(2 * n, 2 * n + 2)
                sp.dma_start(W2[:, two, :, :], c_proj[two].rearrange("e (f p) d -> p e f d", p=P)).then_inc(w2_in, 16)

            def load_w1(n):
                two = slice(2 * n, 2 * n + 2)
                sp.wait_ge(roped, 2 * NB)
                sp.dma_start(W1[:, two, :], c_fc[two].rearrange("e d f -> d e f")).then_inc(w1_in, 16)

            def fill_slots(e):
                sp.wait_ge(dve_const, 2)
                sp.dma_start(slots_x[e * CAP:(e + 1) * CAP, :].rearrange("(p t) d -> p t d", p=P),
                             empty).then_inc(zero_out, 16)

            def fill_parts(n):
                rows = slice(n * CT * P, min((n + 1) * CT, TOPK * NT) * P)
                dst = parts_y[rows, :].rearrange("(t p) d -> p t d", p=P)
                sp.dma_start(dst, empty[:, 0:min(CT, TOPK * NT - n * CT), 0:D]).then_inc(parts_zero, 16)

            loads = [(fill_slots, n) for n in range(E)] + [(load_w2, n) for n in range(E // 2)]
            loads += [(load_w1, n) for n in range(E // 2)] + [(fill_parts, n) for n in range(TOPK * NT // CT + 1)]
            for u in range(2, NU):
                put_negmax(u)
                if u in EXPAND:
                    expand(EXPAND[u])
                if u > max(EXPAND):
                    first = 4 * (u - max(EXPAND) - 1)
                    for load, n in loads[first:first + 4]:
                        load(n)

            sp.wait_ge(scattered, 16 * TOPK * NT)
            for e in range(E):
                if e >= 2:
                    sp.wait_ge(xbt_ps, e - 1)
                    sp.wait_ge(yb_ok, e - 1)
                sp.dma_start(XB[:, e % 2], slots_x[e * CAP:(e + 1) * CAP, :]
                             .rearrange("(t p) d -> p t d", p=P)).then_inc(xb_in[e % 2], 16)
            for i in range(2):
                sp.wait_ge(yb_out[i], 16 * CT * E // 2)
            parts_t = parts_y.ap().rearrange("(k t p) d -> p k t d", k=TOPK, p=P)
            for b in range(NB):
                tiles = slice(TB * b, TB * (b + 1))
                for k in range(TOPK):
                    sp.dma_start(GY[:, k, tiles, :], parts_t[:, k, tiles, :]).then_inc(parts_in[b], 16)
            out_t = out[0].rearrange("(t p) d -> p t d", p=P)
            for b in range(NB):
                sp.wait_ge(out_ok, b + 1)
                sp.dma_start(out_t[:, TB * b:TB * (b + 1), :], X[:, TB * b:TB * (b + 1), :]).then_inc(out_done, 16)
            sp.wait_ge(out_done, 16 * NB)

        @block.gpsimd
        def _(pool):
            g = nc.gpsimd
            n = [0]

            def chain(ins):
                n[0] += 1
                ins.then_inc(pool_step, 1)
                pool.wait_ge(pool_step, n[0])

            g.memset(half[:, :], -0.5).then_inc(pool_step, 1)
            g.memset(ident[:, :], 0.0).then_inc(pool_step, 1)
            g.memset(identb[:, :], 0.0).then_inc(pool_step, 1)
            n[0] = 3
            pool.wait_ge(pool_step, n[0])
            for m in (ident, identb):
                g.affine_select(out=m[:, :], in_=m[:, :], compare_op=ALU.not_equal, fill=1.0, base=0,
                                pattern=[[-1, P]], channel_multiplier=1).then_inc(pool_step, 1)
            n[0] += 2
            pool.wait_ge(pool_step, n[0])
            pool.sem_inc(const_ok, 1)

            def constants():
                g.memset(ones[:, :], 1.0).then_inc(pool_step, 1)
                g.memset(causal[:, :], 0.0).then_inc(pool_step, 1)
                n[0] += 2
                pool.wait_ge(pool_step, n[0])
                g.affine_select(out=causal[:, :], in_=causal[:, :], compare_op=ALU.is_ge, fill=-1e30, base=0,
                                pattern=[[-1, P]], channel_multiplier=1).then_inc(pool_step, 1)
                g.affine_select(out=before[:, :], in_=ones[:, :], compare_op=ALU.is_gt, fill=0.0, base=0,
                                pattern=[[1, P]], channel_multiplier=-1).then_inc(pool_step, 1)
                g.memset(VX[:, :, :, DK:DK + 1], 1.0).then_inc(pool_step, 1)
                n[0] += 3
                chain(g.iota(I8[:, 0, :], pattern=[[1, E]], base=0, channel_multiplier=0))
                chain(g.tensor_copy(io[:, :], I8[:, 0, :]))
                chain(g.iota(row_u[:, :, :], pattern=[[S, TOPK], [P, NT]], base=0, channel_multiplier=1))
                chain(g.tensor_copy(row_id[:, :, :], row_u[:, :, :]))
                chain(g.memset(restart_half[:, :], 1.0))
                chain(g.memset(restart_half[:, :].rearrange("p (n t) -> p n t", t=TB // 2)[:, :, 0:1], 0.0))
                chain(g.memset(restart[:, :], 1.0))
                chain(g.memset(restart[:, :].rearrange("p (n t) -> p n t", t=TB)[:, :, 0:1], 0.0))
                chain(g.tensor_copy(XN[:, :, D], row_id[:, 0, :]))
                pool.sem_inc(const_ok, 1)

            def rstd_of(which, tiles):
                chain(g.tensor_scalar(veps[:, tiles], mv[:, which, tiles, 1], EPS, None, ALU.add))
                g.tensor_tensor(rstd[:, which, tiles], veps[:, tiles], half[:, tiles], ALU.pow).then_inc(rstd_ok, 1)

            gates = 0
            for s in plan:
                if s[0] == "ln":
                    b = s[1]
                    pool.wait_ge(stats_ok, b + 1)
                    rstd_of(0, slice(0, TB) if b == 0 else slice(TB, NT))
                    if b == 0:
                        g.memset(QP[:, 1, :, 0, :].bitcast(f32), 0.0).then_inc(qp_zero, 1)
                        constants()
                        for par in range(2):
                            g.memset(QP[:, par, :, 1, :].bitcast(f32), 0.0).then_inc(qp_zero, 1)
                elif s == ("mod", 1):
                    pool.wait_ge(modb_ok, 1)
                    pool.wait_ge(w_in, 16 * 2)
                    g.tensor_tensor(wsb[:, 3, :], wsb[:, 3, :], MODB[:, 0, :], ALU.mult).then_inc(wo_ok, 1)
                elif s == ("kr", 0):
                    pool.wait_ge(first_part, 2)
                    for t, (_, part) in enumerate(TERMS):
                        if part == 0:
                            pool.dma_start(k_rows[:, DK * t:DK * (t + 1), 0:QB], parts(1, 0, 0)).then_inc(k_first_put, 16)
                elif s[0] == "kr" and s[1] >= 1:
                    b = s[1]
                    pool.wait_ge(roped, 2 * b + 2)
                    if b == 2:
                        pool.wait_ge(k_first_put, 16 * N_FIRST)
                    if b >= 2:
                        pool.wait_ge(qk_put[b - 2], 16 * puts(b - 2))
                    r, d1 = RT[:, 1, 2, :], RT[:, 1, 0, :]
                    chain(g.tensor_scalar(parts(1, b, 0), r, 1.0, 1.0, ALU.mult, ALU.mult))
                    chain(g.tensor_tensor(d1, r, parts(1, b, 0), ALU.subtract))
                    chain(g.tensor_scalar(parts(1, b, 1), d1, 1.0, 1.0, ALU.mult, ALU.mult))
                    chain(g.tensor_tensor(r, d1, parts(1, b, 1), ALU.subtract))
                    g.tensor_scalar(parts(1, b, 2), r, 1.0, 1.0, ALU.mult, ALU.mult).then_inc(kparts_ok, 1)
                elif s[0] == "maxend":
                    u = s[1]
                    pool.wait_ge(mx_ok, u + 1)
                    if u >= 2:
                        pool.wait_ge(mrow_ok, u - 1)
                    chain(g.tensor_scalar(nm[:, u % 2, 0, :], mx[:, u % 2, :], -1.0, 1.0, ALU.mult, ALU.mult))
                    chain(g.tensor_copy(nmp[:, u % 2, 0, :], nm[:, u % 2, 0, :]))
                    chain(g.tensor_tensor(nm[:, u % 2, 1, :], nm[:, u % 2, 0, :], nmp[:, u % 2, 0, :], ALU.subtract))
                    chain(g.tensor_copy(nmp[:, u % 2, 1, :], nm[:, u % 2, 1, :]))
                    chain(g.tensor_tensor(nm[:, u % 2, 2, :], nm[:, u % 2, 1, :], nmp[:, u % 2, 1, :], ALU.subtract))
                    g.tensor_copy(nmp[:, u % 2, 2, :], nm[:, u % 2, 2, :]).then_inc(nmp_ok, 1)
                elif s[0] == "score":
                    _, u, kt, j = s
                    if kt >= TB * units()[u][0]:
                        t = st.tile[u, kt, j]
                        pool.wait_ge(exped, t + 1)
                        tile = PRB[:, t % PR, first_column(u, kt):first_column(u, kt) + P]
                        g.affine_select(out=tile, in_=tile, compare_op=ALU.is_ge, fill=0.0, base=0,
                                        pattern=[[1, P]], channel_multiplier=-1).then_inc(masked, 1)
                    elif u >= 2 * NG and gates < E:
                        if gates == 0:
                            pool.wait_ge(w2_in, 16 * E // 2)
                        g.tensor_tensor(W2[:, gates], W2[:, gates],
                                        MODB[:, 1:2, :].to_broadcast([P, NF, D]), ALU.mult).then_inc(w2_ok, 1)
                        gates += 1
                elif s[0] == "h2":
                    b = s[1]
                    first, nt = BATCHES[b]
                    pool.wait_ge(stats2_ok, first + nt)
                    rstd_of(1, slice(first, first + nt))
                elif s[0] == "h2t":
                    b = s[1]
                    first, nt = BATCHES[b]
                    tiles = slice(first, first + nt)
                    own = slice(on_tile(b, 0), on_tile(b, 0) + nt)
                    if 1 <= b < NB:
                        pool.wait_ge(scattered, 16 * TOPK * first)
                    pool.wait_ge(h2_ok, b + 1)
                    g.tensor_copy(XK[:, own, 0:D], XN[:, tiles, 0:D]).then_inc(xk_ok, 1)
                    g.tensor_copy(XK[:, own, D], row_id[:, 1, tiles]).then_inc(xk_ok, 1)
                elif s[0] == "scatter":
                    _, b, m = s
                    first, nt = BATCHES[b]
                    if m == 0:
                        pool.wait_ge(rows_ok, b + 1)
                        pool.wait_ge(zero_out, 16 * E)
                    if b >= 1 and m == 0:
                        pool.wait_ge(scattered, 16 * (TOPK * first))
                    k, t = 1 - m // nt, m % nt
                    row = XN[:, first + t, :] if k == 0 else XK[:, on_tile(b, t), :]
                    g.indirect_dma_start(out=slots_x[:, :],
                                         out_offset=bass.IndirectOffsetOnAxis(
                                             ap=put_at[:, b % 2, k * nt + t:k * nt + t + 1], axis=0),
                                         in_=row, in_offset=None, bounds_check=NSLOT - 1,
                                         oob_is_err=False).then_inc(scattered, 16)
            pool.wait_ge(parts_zero, 16 * (TOPK * NT // CT + 1))
            for e in range(E):
                if e < E - 1:
                    pool.wait_ge(yb_ok, e + 1)
                for t in range(CT):
                    if e == E - 1:
                        pool.wait_ge(last_ok, t + 1)
                    g.indirect_dma_start(out=parts_y[:, :],
                                         out_offset=bass.IndirectOffsetOnAxis(ap=back_to[:, e, t:t + 1], axis=0),
                                         in_=YB[:, e % 2, t, :], in_offset=None, bounds_check=TOPK * S - 1,
                                         oob_is_err=False).then_inc(yb_out[e % 2], 16)

        @block.scalar
        def _(act):
            a = nc.scalar
            act.wait_ge(mod_in, 16)
            a.activation(ccol[:, 1:2], ccol[:, 0:1], ACT.Exp, scale=-1.0).then_inc(act_silu, 1)
            for s in plan:
                if s[0] == "xt":
                    b = s[1]
                    w = wait_full(act, s)
                    act.wait_ge(modt_ok, 4)
                    a.activation(hT[:, QB * b:QB * (b + 1)], w[:, 0:QB], ACT.Identity, bias=modT[:, 0:1],
                                 scale=modT[:, 1:2]).then_inc(free[ring[s] % NW], 1)
                elif s in (("qr", 0), ("kr", 0)):
                    i = s[0] == "kr"
                    act.wait_ge(roped, 1 + i)
                    a.activation(parts(int(i), 0, 0), RT[:, int(i), 2, :], ACT.Copy).then_inc(first_part, 1)
                    if i:
                        for r in range(1, 3):
                            for i in range(2):
                                act.wait_ge(first_rest, 2 * (r - 1) + i + 1)
                                a.activation(parts(i, 0, r), RT[:, i, (0, 2)[r - 1], :], ACT.Copy).then_inc(first_part, 1)
                elif s[0] == "v":
                    b = s[1]
                    w = wait_full(act, s)
                    act.wait_ge(const_ok, 2)
                    a.activation(VX[:, TB * b:TB * (b + 1), :, 0:DK],
                                 w[:, 0:QB].rearrange("p (t h d) -> p t h d", t=TB, h=H),
                                 ACT.Copy).then_inc(free[ring[s] % NW], 1)
                elif s[0] == "negmax":
                    u = s[1]
                    w = wait_full(act, s)
                    if u >= 2:
                        act.wait_ge(m_put[u % 2], 16 * (u // 2))
                    a.activation(mrow[:, u % 2, :], w[0:3 * GH * TB, 0:P // 2].bitcast(bf16),
                                 ACT.Copy).then_inc(free[ring[s] % NW], 1)
                    wait_read(act, s)
                    act.sem_inc(mrow_ok, 1)
                elif s[0] == "score":
                    _, u, kt, j = s
                    q0 = first_column(u, kt)
                    t = st.tile[u, kt, j]
                    if t >= PR:
                        act.wait_ge(av_ok, (t - PR) // GH + 1)
                    if t == 0:
                        wait_full(act, ("mod", 1))
                    act.wait_ge(scored, t + 1)
                    a.activation(PRB[:, t % PR, q0:QB], SC[t % 3][:, q0:QB], ACT.Exp, scale=SCALE).then_inc(exped, 1)
                    b = units()[u][0] + 2
                    if u % NG == NG - 1 and kt == TB * (b - 1) - 1 and j == GH - 1 and b < NB:
                        act.wait_ge(qk_put[b], 16 * puts(b))
                        for par in range(2):
                            act.dma_start(QP[64 * par:64 * par + ROWS, par, :, b % 2, :],
                                          q_pairs[par, :, :, QB * b:QB * (b + 1)]).then_inc(qk_got[b], 16)
                            act.dma_start(QP[64 * par + ROWS:64 * par + KROWS, par, :, b % 2, :],
                                          pad_t[3:6, 0:NPAIR * QB].rearrange("r (a s) -> r a s", a=NPAIR))\
                               .then_inc(qk_got[b], 16)
                elif s[0] == "evac":
                    u = s[1]
                    b, g = units()[u]
                    before_unit = sum(TB * (bb + 1) for bb, _ in units()[:u])
                    act.wait_ge(av_ok, before_unit + (HALF if u == NU - 1 else TB * (b + 1) - 1) + 1)
                    if b >= 1:
                        wait_full(act, ("norm", b - 1, TB - 1))
                    a.activation(OT[:, g, :], AV[:, :], ACT.Copy).then_inc(evaced, 1)
                elif s[0] == "ot":
                    w = wait_full(act, s)
                    if 1 <= s[1] < NB:
                        wait_full(act, ("wo", s[1] - 1))
                    wide = P * BATCHES[s[1]][1]
                    half_at = QB // 2 * (s[1] == NB)
                    a.activation(OnT[:, half_at:half_at + wide], w[:, 0:wide], ACT.Copy).then_inc(free[ring[s] % NW], 1)
                elif s[0] == "h2t":
                    w = wait_full(act, s)
                    first, wide = (P * n for n in BATCHES[s[1]])
                    a.activation(hT[:, first:first + wide], w[:, 0:wide], ACT.Identity, bias=modT[:, 2:3],
                                 scale=modT[:, 3:4]).then_inc(free[ring[s] % NW], 1)
                elif s[0] == "rank":
                    act.wait_ge(diff_ok, s[1] + 1)
                    n = BATCHES[s[1]][1]
                    a.activation(wt[:, 1, 0:n], wt[:, 0, 0:n], ACT.Exp).then_inc(ediff_ok, 1)
            for e in range(E):
                for f in range(NF):
                    m = e * NF + f
                    act.wait_ge(up_full[m % 2], m // 2 + 1)
                    if e >= 2 and f == 0:
                        act.wait_ge(down_ps, e - 1)
                    a.activation(HG[:, e % 2, f, :].rearrange("p (n s) -> p n s", n=2),
                                 WK[:, 2 * (m % 2):2 * (m % 2) + 2, 0:CAP // 2],
                                 ACT.Gelu).then_inc(up_free[m % 2], 1)

        @block.vector
        def _(dve):
            v = nc.vector
            n = [0]

            def chain(ins):
                n[0] += 1
                ins.then_inc(dve_step, 1)
                dve.wait_ge(dve_step, n[0])

            for s in plan:
                kind = s[0]
                if kind in ("ln", "xn"):
                    b = s[1]
                    if kind == "ln":
                        known = range(0, TB) if b == 0 else range(TB, NT)
                        for t in known:
                            if t % TB == 0:
                                dve.wait_ge(x_in[t // TB], 16)
                            v.bn_stats(stats[:, t, :], X[:, t, :]).then_inc(dve_step, 1)
                        n[0] += len(known)
                        dve.wait_ge(dve_step, n[0])
                        for t in known:
                            v.bn_aggr(mv[:, 0, t, :], stats[:, t, :]).then_inc(dve_step, 1)
                        n[0] += len(known)
                        dve.wait_ge(dve_step, n[0])
                        dve.sem_inc(stats_ok, 1)
                    if kind == "xn" or b == 0:
                        dve.wait_ge(rstd_ok, min(b, 1) + 1)
                    for t in range(TB * b, TB * (b + 1)) if kind == "xn" or b == 0 else ():
                        v.tensor_scalar(XN[:, t, 0:D], X[:, t, :], mv[:, 0, t, 0:1], rstd[:, 0, t:t + 1],
                                        ALU.subtract, ALU.mult).then_inc(xn_ok, 1)
                    if b == 0:
                        dve.wait_ge(act_silu, 1)
                        chain(v.tensor_scalar(ccol[:, 2:3], ccol[:, 1:2], 1.0, None, ALU.add))
                        chain(v.reciprocal(ccol[:, 3:4], ccol[:, 2:3]))
                        chain(v.tensor_tensor(ccol[:, 1:2], ccol[:, 0:1], ccol[:, 3:4], ALU.mult))
                        v.tensor_copy(silu_b[:, :], ccol[:, 1:2].to_broadcast([P, P])).then_inc(silu_ok, 1)
                        dve.wait_ge(wqk_in, 16 * 2)
                        for i in range(2):
                            src = wsb[:, i, :].rearrange("p (n two) -> p n two", two=2)
                            dst = wsb[:, 4 + i, :].rearrange("p (n two) -> p n two", two=2)
                            v.tensor_scalar(dst[:, :, 0], src[:, :, 1], -1.0, None, ALU.mult).then_inc(rot_ok, 1)
                            v.tensor_copy(dst[:, :, 1], src[:, :, 0]).then_inc(rot_ok, 1)
                elif kind == "mod":
                    w = wait_full(dve, s)
                    if s[1] == 0:
                        for i in range(2):
                            v.tensor_copy(modT[:, 2 * i:2 * i + 1], w[:, 2 * i:2 * i + 1]).then_inc(modt_ok, 1)
                            v.tensor_scalar(modT[:, 2 * i + 1:2 * i + 2], w[:, 2 * i + 1:2 * i + 2],
                                            1.0, None, ALU.add).then_inc(modt_ok, 1)
                        dve.wait_ge(modt_ok, 4)
                        release(dve, s)
                        continue
                    for i in range(2):
                        chain(v.tensor_copy(MODB[:, i, :], w[:, i * D:(i + 1) * D]))
                        chain(v.tensor_scalar(sign[:, :], MODB[:, i, :], 0.0, 2.0, ALU.is_ge, ALU.mult))
                        chain(v.tensor_scalar(sign[:, :], sign[:, :], -1.0, None, ALU.add))
                        chain(v.tensor_tensor(MODB[:, i, :], MODB[:, i, :], sign[:, :], ALU.mult))
                        chain(v.tensor_scalar(MODB[:, i, :], MODB[:, i, :], 0.25, None, ALU.max))
                        chain(v.tensor_tensor(MODB[:, i, :], MODB[:, i, :], sign[:, :], ALU.mult))
                    release(dve, s)
                    dve.sem_inc(modb_ok, 1)
                elif kind in ("q", "k"):
                    b, i = s[1], kind == "k"
                    w = wait_full(dve, s)
                    dve.wait_ge(rope_in[b], 32)
                    if b == 1:
                        dve.wait_ge(first_part, 6)
                    elif i and b:
                        dve.wait_ge(kparts_ok, b - 1)
                    v.tensor_tensor(RT[:, i, 0, :], w, CS[:, 0, QB * b:QB * (b + 1)],
                                    ALU.mult).then_inc(free[ring[s] % NW], 1)
                elif kind in ("qr", "kr"):
                    b, i = s[1], kind == "kr"
                    w = wait_full(dve, s)
                    v.tensor_tensor(RT[:, i, 1, :], w, CS[:, 1, QB * b:QB * (b + 1)],
                                    ALU.mult).then_inc(free[ring[s] % NW], 1)
                    wait_read(dve, s)
                    r, d1 = RT[:, i, 2, :], RT[:, i, 0, :]
                    v.tensor_tensor(r, RT[:, i, 0, :], RT[:, i, 1, :], ALU.add).then_inc(roped, 1)
                    if b == 0:
                        if i:
                            for r in range(2):
                                for i in range(2):
                                    src, dst = RT[:, i, (2, 0)[r], :], RT[:, i, (0, 2)[r], :]
                                    dve.wait_ge(first_part, 2 * r + i + 1)
                                    v.tensor_tensor(dst, src, parts(i, 0, r), ALU.subtract).then_inc(first_rest, 1)
                            v.memset(QP[:, 0, :, 0, :].bitcast(f32), 0.0).then_inc(qp_zero, 1)
                            v.memset(AV[:, :], 0.0).then_inc(dve_const, 1)
                    elif not i:
                        dve.wait_ge(roped, 2 * b + 1)
                        if b >= 2:
                            dve.wait_ge(qk_put[b - 2], 16 * puts(b - 2))
                        chain(v.tensor_copy(parts(0, b, 0), r))
                        chain(v.tensor_tensor(d1, r, parts(0, b, 0), ALU.subtract))
                        chain(v.tensor_copy(parts(0, b, 1), d1))
                        chain(v.tensor_tensor(r, d1, parts(0, b, 1), ALU.subtract))
                        v.tensor_copy(parts(0, b, 2), r).then_inc(qparts_ok, 1)
                        dve.wait_ge(qparts_ok, b)
                elif s == ("v", NB - 1):
                    dve.wait_ge(kparts_ok, NB - 1)
                    chain(v.memset(empty, 0.0))
                    v.memset(empty[:, :, D:D + 1], NOWHERE).then_inc(dve_const, 1)
                elif kind == "max":
                    _, u, m = s
                    heads, i, k0, keys = max_pieces(u)[m]
                    w = wait_full(dve, s)
                    cols = slice(heads[0] * TB + i % TB, heads[-1] * TB + i % TB + 1, TB)
                    v.tensor_reduce(mpart[:, u % 2, cols, k0 // QB],
                                    w[:, 0:len(heads) * keys].rearrange("p (j k) -> p j k", k=keys),
                                    AX.X, ALU.max).then_inc(free[ring[s] % NW], 1)
                elif kind == "maxend":
                    u = s[1]
                    wait_read(dve, ("max", u, len(max_pieces(u)) - 1))
                    if u >= 2:
                        dve.wait_ge(nmp_ok, u - 1)
                    v.tensor_reduce(mx[:, u % 2, :], mpart[:, u % 2, :, 0:units()[u][0] + 1], AX.X,
                                    ALU.max).then_inc(mx_ok, 1)
                elif kind == "tail":
                    w = wait_full(dve, s)
                    dve.wait_ge(evaced, NU)
                    second = OT[:, NG - 1, QB // 2:QB]
                    v.tensor_tensor(second, second, w[:, QB // 2:QB], ALU.add).then_inc(free[ring[s] % NW], 1)
                elif kind == "norm":
                    _, b, t = s
                    w = wait_full(dve, s)
                    strips = w.rearrange("p (h r) -> p h r", h=H)
                    if t == 0 and 1 <= b < NB:
                        wait_full(dve, ("ot", b - 1))
                    chain(v.reciprocal(rl[:, t % 2, :], strips[:, :, DK]))
                    v.tensor_tensor(On[:, on_tile(b, t), :].rearrange("p (h d) -> p h d", h=H), strips[:, :, 0:DK],
                                    rl[:, t % 2, :].rearrange("p (h o) -> p h o", o=1).to_broadcast([P, H, DK]),
                                    ALU.mult).then_inc(free[ring[s] % NW], 1)
                elif kind == "wo":
                    b = s[1]
                    first, nt = BATCHES[b]
                    tiles = slice(first, first + nt)
                    w = wait_full(dve, s)
                    v.tensor_tensor(X[:, tiles, :], w[:, 0:nt * D].rearrange("p (t d) -> p t d", t=nt), X[:, tiles, :],
                                    ALU.add).then_inc(free[ring[s] % NW], 1)
                    wait_read(dve, s)
                    for t in range(first, first + nt):
                        v.bn_stats(stats[:, t, :], X[:, t, :]).then_inc(dve_step, 1)
                    n[0] += nt
                    dve.wait_ge(dve_step, n[0])
                    for t in range(first, first + nt):
                        v.bn_aggr(mv[:, 1, t, :], stats[:, t, :]).then_inc(stats2_ok, 1)
                elif kind == "h2":
                    b = s[1]
                    first, nt = BATCHES[b]
                    dve.wait_ge(rstd_ok, 2 + b + 1)
                    wait_full(dve, ("xt", first // TB))
                    for t in range(first, first + nt):
                        last = v.tensor_scalar(XN[:, t, 0:D], X[:, t, :], mv[:, 1, t, 0:1], rstd[:, 1, t:t + 1],
                                               ALU.subtract, ALU.mult)
                    last.then_inc(h2_ok, 1)
                elif kind == "logit":
                    b = s[1]
                    first, nt = BATCHES[b]
                    w = wait_full(dve, s)
                    chain(v.tensor_copy(LG[:, 0:nt, :], w[:, 0:nt * E].rearrange("p (t e) -> p t e", t=nt)))
                    release(dve, s)
                    for t in range(nt):
                        v.max(T8[:, t, :], LG[:, t, :]).then_inc(dve_step, 1)
                    n[0] += nt
                    dve.wait_ge(dve_step, n[0])
                    v.tensor_tensor(wt[:, 0, 0:nt], T8[:, 0:nt, 1], T8[:, 0:nt, 0], ALU.subtract).then_inc(diff_ok, 1)
                    for t in range(nt):
                        v.max_index(I8[:, t, :], T8[:, t, :], LG[:, t, :]).then_inc(dve_step, 1)
                    n[0] += nt
                    dve.wait_ge(dve_step, n[0])
                    idx = idx_s[:, 0:TOPK * nt]
                    chain(v.tensor_copy(idx.rearrange("p (k t) -> p k t", k=TOPK),
                                        I8[:, 0:nt, 0:TOPK].rearrange("p t k -> p k t")))
                    v.tensor_tensor(OH_s[:, 0:E * TOPK * nt].rearrange("p (e n) -> p e n", e=E),
                                    idx.rearrange("p (o n) -> p o n", o=1).to_broadcast([P, E, TOPK * nt]),
                                    io[:, :].rearrange("p (e o) -> p e o", o=1).to_broadcast([P, E, TOPK * nt]),
                                    ALU.is_equal).then_inc(oh_ok, 1)
                elif kind == "rank":
                    b = s[1]
                    first_tile, nt = BATCHES[b]
                    tiles = slice(first_tile, first_tile + nt)
                    own = slice(on_tile(b, 0), on_tile(b, 0) + nt)
                    w = wait_full(dve, s)
                    flat_n = E * TOPK * nt
                    local, total = w[:, 0:flat_n], w[:, flat_n:2 * flat_n]
                    fl, earlier, oh = incl_s[:, 0:flat_n], before_s[:, 0:flat_n], OH_s[:, 0:flat_n]
                    incl = fl.rearrange("p (e k t) -> p e k t", e=E, k=TOPK)
                    choice = oh.rearrange("p (e k t) -> p e k t", e=E, k=TOPK)
                    first = first_s[:, 0:E * nt].rearrange("p (e t) -> p e t", e=E)
                    idx, rk, keep = (x[:, 0:TOPK * nt].rearrange("p (k t) -> p k t", k=TOPK)
                                     for x in (idx_s, rk_s, keep_s))
                    slotf = [slot_s[:, i, 0:TOPK * nt].rearrange("p (k t) -> p k t", k=TOPK) for i in range(3)]
                    chain(v.tensor_tensor_scan(fl, (restart if nt == TB else restart_half)[:, 0:flat_n], total, 0.0,
                                               ALU.mult, ALU.add))
                    if b >= 1:
                        chain(v.tensor_tensor(incl, incl, count[:, :, :].rearrange("p e (k o) -> p e k o", o=1)
                                              .to_broadcast([P, E, TOPK, nt]), ALU.add))
                    v.tensor_copy(count[:, :, :], incl[:, :, :, nt - 1]).then_inc(dve_step, 1)
                    v.tensor_tensor(earlier, fl, total, ALU.subtract).then_inc(dve_step, 1)
                    n[0] += 2
                    dve.wait_ge(dve_step, n[0])
                    chain(v.tensor_tensor(earlier, earlier, local, ALU.add))
                    release(dve, s)
                    chain(v.tensor_tensor(earlier, earlier, oh, ALU.mult))
                    v.tensor_reduce(rk_s[:, 0:TOPK * nt], earlier.rearrange("p (e n) -> p n e", e=E), AX.X,
                                    ALU.add).then_inc(dve_step, 1)
                    v.tensor_tensor(first, choice[:, :, 1, :], count[:, :, 0:1].to_broadcast([P, E, nt]),
                                    ALU.mult).then_inc(dve_step, 1)
                    n[0] += 2
                    dve.wait_ge(dve_step, n[0])
                    chain(v.tensor_reduce(taken[:, 0:nt], first.rearrange("p e t -> p t e"), AX.X, ALU.add))
                    v.tensor_scalar(keep[:, 0, :], rk[:, 0, :], float(CAP), None, ALU.is_lt).then_inc(dve_step, 1)
                    v.tensor_tensor(taken[:, 0:nt], taken[:, 0:nt], rk[:, 1, :], ALU.add).then_inc(dve_step, 1)
                    v.scalar_tensor_tensor(slotf[0][:, 0, :], idx[:, 0, :], float(CAP), rk[:, 0, :],
                                           ALU.mult, ALU.add).then_inc(dve_step, 1)
                    v.scalar_tensor_tensor(slotf[0][:, 1, :], idx[:, 1, :], float(CAP), rk[:, 1, :],
                                           ALU.mult, ALU.subtract).then_inc(dve_step, 1)
                    n[0] += 4
                    dve.wait_ge(dve_step, n[0])
                    v.tensor_scalar(keep[:, 1, :], taken[:, 0:nt], float(CAP), None, ALU.is_lt).then_inc(dve_step, 1)
                    v.tensor_scalar(slotf[1][:, 0, :], slotf[0][:, 0, :], NOWHERE, None, ALU.add).then_inc(dve_step, 1)
                    v.tensor_scalar(slotf[1][:, 1, :], slotf[0][:, 1, :], NOWHERE + CAP - 1, None,
                                    ALU.add).then_inc(dve_step, 1)
                    n[0] += 3
                    dve.wait_ge(dve_step, n[0])
                    chain(v.scalar_tensor_tensor(slot_s[:, 2, 0:TOPK * nt], keep_s[:, 0:TOPK * nt], -NOWHERE,
                                                 slot_s[:, 1, 0:TOPK * nt], ALU.mult, ALU.add))
                    if b >= 2:
                        dve.wait_ge(scattered, 16 * TOPK * BATCHES[b - 1][0])
                    v.tensor_copy(put_at[:, b % 2, 0:TOPK * nt], slot_s[:, 2, 0:TOPK * nt]).then_inc(dve_step, 1)
                    n[0] += 1
                    dve.wait_ge(ediff_ok, b + 1)
                    dve.wait_ge(xk_ok, 2 * (b + 1))
                    chain(v.tensor_scalar(wt[:, 2, 0:nt], wt[:, 1, 0:nt], 1.0, None, ALU.add))
                    chain(v.reciprocal(XN[:, tiles, D + 1], wt[:, 2, 0:nt]))
                    chain(v.tensor_tensor(XK[:, own, D + 1], XN[:, tiles, D + 1], wt[:, 1, 0:nt], ALU.mult))
                    dve.sem_inc(rows_ok, 1)

            for e in range(E + 1):
                if e < E:
                    dve.wait_ge(xbt_ps, e + 1)
                    if e >= 2:
                        for i in range(2):
                            dve.wait_ge(up_full[i], (e - 1) * NF // 2)
                    v.tensor_scalar(XBT[:, e % 2, 0:QB], SC[0][:, :], modT[:, 3:4], modT[:, 2:3],
                                    ALU.mult, ALU.add).then_inc(xbt_ok, 1)
                    v.tensor_scalar(XBT[:, e % 2, QB:CAP], SC[1][:, 0:CAP - QB], modT[:, 3:4], modT[:, 2:3],
                                    ALU.mult, ALU.add).then_inc(xbt_ok, 1)
                    dve.wait_ge(xb_in[e % 2], 16 * (e // 2 + 1))
                    v.tensor_copy(back_to[:, e, :], XB[:, e % 2, :, D]).then_inc(dve_step, 1)
                    n[0] += 1
                if e == E:
                    dve.wait_ge(yb_out[(E - 1) % 2], 16 * CT * ((E - 1) // 2))
                    for t in range(CT):
                        dve.wait_ge(last_ps, t + 1)
                        v.tensor_tensor(YB[:, (E - 1) % 2, t, :], last_bank(t),
                                        XB[:, (E - 1) % 2, t, D + 1:D + 2].to_broadcast([P, D]),
                                        ALU.mult).then_inc(last_ok, 1)
                elif e >= 1:
                    f = e - 1
                    dve.wait_ge(down_ps, f + 1)
                    if f >= 2:
                        dve.wait_ge(yb_out[f % 2], 16 * CT * (f // 2))
                    v.tensor_tensor(YB[:, f % 2, 0:4, :], AV[:, :].rearrange("p (t d) -> p t d", t=4),
                                    XB[:, f % 2, 0:4, D + 1:D + 2].to_broadcast([P, 4, D]), ALU.mult).then_inc(dve_step, 1)
                    v.tensor_tensor(YB[:, f % 2, 4, :], SC[2][:, 0:D],
                                    XB[:, f % 2, 4, D + 1:D + 2].to_broadcast([P, D]), ALU.mult).then_inc(dve_step, 1)
                    n[0] += 2
                    dve.wait_ge(dve_step, n[0])
                    dve.sem_inc(yb_ok, 1)
            for b in range(NB):
                tiles = slice(TB * b, TB * (b + 1))
                dve.wait_ge(parts_in[b], 16 * TOPK)
                chain(v.tensor_tensor(X[:, tiles, :], X[:, tiles, :], GY[:, 0, tiles, :], ALU.add))
                v.tensor_tensor(X[:, tiles, :], X[:, tiles, :], GY[:, 1, tiles, :], ALU.add).then_inc(out_ok, 1)

        @block.tensor
        def _(pe):
            t_ = nc.tensor

            def take(step):
                r = ring[step]
                if r >= NW:
                    pe.wait_ge(free[r % NW], r // NW)
                return WK[:, r % NW, :], full[r % NW]

            pe.wait_ge(const_ok, 1)
            for s in plan:
                kind = s[0]
                if kind == "mod":
                    w, ok = take(s)
                    pe.wait_ge(silu_ok, 1)
                    pe.wait_ge(wm_in, 16)
                    if s[1] == 0:
                        for n, i in enumerate((0, 1, 3, 4)):
                            last = t_.matmul(w[:, n:n + 1], wm[:, i * D:(i + 1) * D], silu_b[:, 0:1],
                                             start=True, stop=True)
                    else:
                        for n, i in enumerate((2, 5)):
                            last = t_.matmul(w[:, n * D:(n + 1) * D], silu_b[:, :], wm[:, i * D:(i + 1) * D],
                                             start=True, stop=True)
                    last.then_inc(ok, 1)
                elif kind == "xt":
                    b = s[1]
                    w, ok = take(s)
                    pe.wait_ge(xn_ok, TB * (b + 1))
                    for t in range(TB):
                        last = t_.transpose(w[:, t * P:(t + 1) * P], XN[:, TB * b + t, 0:D], ident[:, :])
                    last.then_inc(ok, 1)
                elif kind in ("q", "k", "qr", "kr"):
                    b = s[1]
                    w, ok = take(s)
                    wait_read(pe, ("xt", b))
                    pe.wait_ge(rot_ok, 4)
                    t_.matmul(w, wsb[:, {"q": 0, "k": 1, "qr": 4, "kr": 5}[kind], :], hT[:, QB * b:QB * (b + 1)],
                              start=True, stop=True).then_inc(ok, 1)
                elif kind == "v":
                    b = s[1]
                    w, ok = take(s)
                    pe.wait_ge(w_in, 16 * 2)
                    for t in range(TB):
                        last = t_.matmul(w[:, t * P:(t + 1) * P], hT[:, (TB * b + t) * P:(TB * b + t + 1) * P],
                                         wsb[:, 2, :], start=True, stop=True)
                    last.then_inc(ok, 1)
                elif kind == "max":
                    _, u, m = s
                    b, g = units()[u]
                    heads, i, k0, keys = max_pieces(u)[m]
                    w, ok = take(s)
                    if u == 0 and m == 0:
                        pe.wait_ge(ones_in, 32)
                        pe.wait_ge(const_ok, 2)
                    if m == 0 and g == 0:
                        pe.wait_ge(qk_got[b], 16 * (4 if b < 2 else 6))
                    if m == 0 and g == NG // 2:
                        pe.wait_ge(qk_more[b], 16 * (4 if b < 2 else 2))
                    ends = k0 + keys == P * (i + 1)
                    for n, j in enumerate(heads):
                        h = GH * g + j
                        row = w[:, n * keys:(n + 1) * keys]
                        last = t_.matmul(row, QP[:, h % 2, h // 2, b % 2, (i % TB) * P:(i % TB + 1) * P],
                                         KS[:, h // 2, k0:k0 + keys], start=True, stop=not ends)
                        if ends:
                            last = t_.matmul(row[:, keys - P:keys], identb[:, :], causal[:, :],
                                             start=False, stop=True)
                    last.then_inc(ok, 1)
                elif kind == "negmax":
                    u = s[1]
                    w, ok = take(s)
                    pe.wait_ge(nmp_ok, u + 1)
                    t_.transpose(w[0:3 * GH * TB, 0:P // 2].bitcast(bf16),
                                 nmp[:, u % 2, :, :].rearrange("p r n -> p (r n)"), identb[:, :]).then_inc(ok, 1)
                elif kind == "score":
                    _, u, kt, j = s
                    b, g = units()[u]
                    q0 = first_column(u, kt)
                    if kt == 0 and j == 0:
                        pe.wait_ge(m_got[u % 2], 32 * (u // 2 + 1))
                    h = GH * g + j
                    t = st.tile[u, kt, j]
                    if t >= 3:
                        pe.wait_ge(exped, t - 2)
                    t_.matmul(SC[t % 3][:, q0:QB], KS[:, h // 2, kt * P:(kt + 1) * P],
                              QP[:, h % 2, h // 2, b % 2, q0:QB], start=True, stop=True).then_inc(scored, 1)
                elif kind == "av":
                    _, u, kt = s
                    b, g = units()[u]
                    q0 = first_column(u, kt)
                    pe.wait_ge(exped, st.tile[u, kt, GH - 1] + 1)
                    if (u, kt, GH - 1) in st.diag:
                        pe.wait_ge(masked, st.diag[u, kt, GH - 1])
                    if u == 0 and kt == 0:
                        pe.wait_ge(dve_const, 1)
                    if g == 0 and kt == TB * b:
                        wait_read(pe, ("v", b))
                    if kt == 0 and u >= 1:
                        pe.wait_ge(evaced, u)
                    for j in range(GH):
                        last = t_.matmul(AV[32 * j:32 * j + DK + 1, q0:QB], VX[:, kt, GH * g + j, :],
                                         PRB[:, st.tile[u, kt, j] % PR, q0:QB], start=(kt == 0),
                                         stop=(kt == (HALF if u == NU - 1 else TB * (b + 1) - 1)))
                    last.then_inc(av_ok, 1)
                elif kind == "tail":
                    w, ok = take(s)
                    tail = range(HALF + 1, NT)
                    pe.wait_ge(exped, len(st.tile))
                    pe.wait_ge(masked, len(st.diag))
                    for kt in tail:
                        q0 = first_column(NU - 1, kt)
                        for j in range(GH):
                            last = t_.matmul(w[32 * j:32 * j + DK + 1, q0:QB], VX[:, kt, H - GH + j, :],
                                             PRB[:, st.tile[NU - 1, kt, j] % PR, q0:QB], start=(kt == tail[0]),
                                             stop=(kt == tail[-1]))
                    last.then_inc(ok, 1)
                elif kind == "norm":
                    _, b, t = s
                    w, ok = take(s)
                    pe.wait_ge(evaced, min(NG * (b + 1), NU))
                    if b == NB:
                        wait_read(pe, ("tail", 0))
                    q = (BATCHES[b][0] + t) % TB * P
                    for g in range(NG):
                        last = t_.transpose(w[:, g * P:(g + 1) * P], OT[:, g, q:q + P], ident[:, :])
                    last.then_inc(ok, 1)
                elif kind == "ot":
                    b = s[1]
                    w, ok = take(s)
                    for t in range(BATCHES[b][1]):
                        wait_read(pe, ("norm", b, t))
                        last = t_.transpose(w[:, t * P:(t + 1) * P], On[:, on_tile(b, t), :], ident[:, :])
                    last.then_inc(ok, 1)
                elif kind == "wo":
                    b = s[1]
                    w, ok = take(s)
                    wait_read(pe, ("ot", b))
                    pe.wait_ge(wo_ok, 1)
                    for t in range(BATCHES[b][1]):
                        last = t_.matmul(w[:, t * P:(t + 1) * P], OnT[:, on_tile(b, t) * P:(on_tile(b, t) + 1) * P], wsb[:, 3, :],
                                         start=True, stop=True)
                    last.then_inc(ok, 1)
                elif kind == "h2t":
                    b = s[1]
                    w, ok = take(s)
                    pe.wait_ge(h2_ok, b + 1)
                    for t in range(BATCHES[b][1]):
                        last = t_.transpose(w[:, t * P:(t + 1) * P], XN[:, BATCHES[b][0] + t, 0:D], ident[:, :])
                    last.then_inc(ok, 1)
                elif kind == "logit":
                    b = s[1]
                    w, ok = take(s)
                    wait_read(pe, ("h2t", b))
                    pe.wait_ge(wg_in, 16)
                    for t in range(BATCHES[b][1]):
                        last = t_.matmul(w[:, t * E:(t + 1) * E], hT[:, (BATCHES[b][0] + t) * P:(BATCHES[b][0] + t + 1) * P],
                                         wg[:, :], start=True, stop=True)
                    last.then_inc(ok, 1)
                elif kind == "rank":
                    w, ok = take(s)
                    pe.wait_ge(oh_ok, s[1] + 1)
                    n_oh = E * TOPK * BATCHES[s[1]][1]
                    oh = OH_s[:, 0:n_oh]
                    t_.matmul(w[:, 0:n_oh], before[:, :], oh, start=True, stop=True)
                    t_.matmul(w[:, n_oh:2 * n_oh], ones[:, :], oh, start=True, stop=True).then_inc(ok, 1)

            def turn(e):
                pe.wait_ge(xb_in[e % 2], 16 * (e // 2 + 1))
                if e == 0:
                    pe.wait_ge(exped, len(st.tile))
                else:
                    pe.wait_ge(xbt_ok, 2 * e)
                for t in range(CT):
                    dst = SC[0][:, t * P:(t + 1) * P] if t < 4 else SC[1][:, 0:P]
                    last = t_.transpose(dst, XB[:, e % 2, t, 0:D], ident[:, :])
                last.then_inc(xbt_ps, 1)

            for r in range(NRING - NW, NRING):
                pe.wait_ge(free[r % NW], r // NW + 1)
            pe.wait_ge(w1_in, 16 * E // 2)
            pe.wait_ge(w2_ok, E)
            pe.wait_ge(evaced, NU)
            turn(0)
            for e in range(E):
                pe.wait_ge(xbt_ok, 2 * (e + 1))
                for f in range(NF):
                    m = e * NF + f
                    if m >= 2:
                        pe.wait_ge(up_free[m % 2], m // 2)
                    for i in range(2):
                        last = t_.matmul(WK[:, 2 * (m % 2) + i, 0:CAP // 2], W1[:, e, f * P:(f + 1) * P],
                                         XBT[:, e % 2, i * CAP // 2:(i + 1) * CAP // 2], start=True, stop=True)
                    last.then_inc(up_full[m % 2], 1)
                if e + 1 < E:
                    turn(e + 1)
                for i in range(2):
                    pe.wait_ge(up_free[i], (e + 1) * NF // 2)
                if e >= 1:
                    pe.wait_ge(yb_ok, e)
                for t in range(CT):
                    dst = AV[:, t * D:(t + 1) * D] if t < 4 else SC[2][:, 0:D]
                    if e == E - 1:
                        dst = last_bank(t)
                    for f in range(NF):
                        last = t_.matmul(dst, HG[:, e % 2, f, t * P:(t + 1) * P], W2[:, e, f, :],
                                         start=(f == 0), stop=(f == NF - 1))
                    if e == E - 1:
                        last.then_inc(last_ps, 1)
                if e < E - 1:
                    last.then_inc(down_ps, 1)


_INS = ["L0_attn_x", "L0_attn_Wq", "L0_attn_Wk", "L0_attn_Wv", "L0_attn_Wo", "L0_ffn_w_g", "L0_ffn_c_fc",
        "L0_ffn_c_proj", "L0_c", "L0_wmod"]


def rotary_tables():
    inv = (1.0 / np.float32(10000.0) ** (np.arange(0, DK, 2, dtype=np.float32) / np.float32(DK))).astype(np.float32)
    ang = np.outer(np.arange(S, dtype=np.float32), inv).astype(np.float32)
    cos, sin = (np.repeat(f(ang).astype(np.float32), 2, axis=-1).T for f in (np.cos, np.sin))
    return np.ascontiguousarray(np.tile(cos, (H, 1))), np.ascontiguousarray(np.tile(sin, (H, 1)))


def kernel(**inputs):
    import concourse.bacc as _bacc
    from concourse import mybir as _mybir
    from concourse.bass_utils import run_bass_kernel_spmd as _run

    nc = _bacc.Bacc("TRN2", target_bir_lowering=False, num_devices=1)
    arrays, args = {}, []
    for name in _INS:
        arrays[f"in_{name}_dram"] = np.ascontiguousarray(inputs[name])
    arrays["rope_cos"], arrays["rope_sin"] = rotary_tables()
    import ml_dtypes
    pad = np.zeros((64 - ROWS, NPAIR * S), ml_dtypes.bfloat16)
    pad[0:3] = 1.0
    arrays["pad_rows"] = pad
    for name, a in arrays.items():
        args.append(nc.dram_tensor(name, a.shape, _mybir.dt.from_np(a.dtype), kind="ExternalInput").ap())
    args.append(nc.dram_tensor("out_dram", (1, S, D), _mybir.dt.float32, kind="ExternalOutput").ap())
    block_kernel(nc, *args)
    r = _run(nc, [arrays], core_ids=[0])
    return r.results[0]["out_dram"]
```
